# Optimizing a Trainium2 kernel written in Bass

```python
import numpy as np
import jax
import jax.numpy as jnp

def _softmax(x, axis=-1):
    return jax.nn.softmax(x, axis=axis)

def _gelu(x):
    return jax.nn.gelu(x, approximate=True)

def _silu(x):
    return jax.nn.silu(x)

def _sigmoid(x):
    return jax.nn.sigmoid(x)

def _layernorm(x, axis=-1, eps=1e-05):
    m = jnp.mean(x, axis=axis, keepdims=True)
    v = jnp.var(x, axis=axis, keepdims=True)
    return (x - m) / jnp.sqrt(v + eps)

def _scatter_add(tgt, idx, src, axis=0):
    return tgt.at[idx].add(src)

def _segment_sum(src, seg, n):
    return jax.ops.segment_sum(src, seg, n)
kernel_name = 'mk_xattn_ffn_d2_seqx_r8_d7d098'

def setup_inputs(seed: int=0):
    np.random.seed(seed)
    _w = jnp.asarray

    def _rec_inputs():
        import jax
        import jax.numpy as jnp
        _rk = jax.random.key(seed)
        x = -0.0002928 + 1 * jax.random.normal(jax.random.fold_in(_rk, 1), (8, 128, 512), jnp.float32)
        _lenS = 128 - jax.random.randint(jax.random.fold_in(_rk, 7), (8,), 0, max(1, 128 // 4) + 1, jnp.int32)
        _lenS2 = 128 - jax.random.randint(jax.random.fold_in(_rk, 8), (8,), 0, max(1, 128 // 4) + 1, jnp.int32)
        _ctx_4096P = jax.random.normal(jax.random.fold_in(_rk, 11), (8, 16, 512), jnp.float32)
        _ctx_4096c = jax.random.dirichlet(jax.random.fold_in(_rk, 511), 0.3 * jnp.ones((16,), jnp.float32), (8, 128))
        _ctx_4096t = jnp.einsum('bsk,bkd->bsd', _ctx_4096c, _ctx_4096P)
        _ctx_4096t = _ctx_4096t * jax.lax.rsqrt(jnp.mean(jnp.square(_ctx_4096t)) + 1e-12) * 0.953939
        ctx_4096 = -2.8382e-05 + 0.999851 * (_ctx_4096t + 0.3 * jax.random.normal(jax.random.fold_in(_rk, 611), (8, 128, 512), jnp.float32))
        _validS = jnp.arange(128)[None, :] < _lenS[:, None]
        _validS2 = jnp.arange(128)[None, :] < _lenS2[:, None]
        _causal = jnp.tril(jnp.ones((128, 128), dtype=bool))
        mask_1x1xSxS2_ff0 = jnp.where(jnp.ones((1, 1, 128, 128), dtype=bool), 0.0, -1000000000.0).astype(jnp.float32)
        mask_BxSxS2_bk0 = jnp.logical_not(jnp.broadcast_to(_validS2[:, None, :], (8, 128, 128)))
        return (x, ctx_4096, mask_1x1xSxS2_ff0, mask_BxSxS2_bk0)
    x, ctx_4096, mask_1x1xSxS2_ff0, mask_BxSxS2_bk0 = _rec_inputs()

    def _L0_xattn_setup():
        import jax, jax.numpy as jnp
        import numpy as np
        B, Q, K, D = (1, 128, 6404, 512)
        H, KVH, HD = (32, 8, 128)
        GROUPS = H // KVH
        EPS = 1e-05

        def _rmsnorm(x, w):
            xf = x.astype(jnp.float32)
            var = jnp.mean(xf * xf, axis=-1, keepdims=True)
            return (xf * jax.lax.rsqrt(var + EPS)).astype(x.dtype) * w
        key = jax.random.key(seed)
        ks = jax.random.split(key, 8)
        s = 0.02
        return {'hidden_states': jax.random.normal(ks[0], (B, Q, D), jnp.float32), 'cross_attention_states': jax.random.normal(ks[1], (B, K, D), jnp.float32), 'attention_mask': jnp.zeros((B, 1, Q, K), jnp.float32), 'Wq': jax.random.normal(ks[2], (H * HD, D), jnp.float32) * s, 'Wk': jax.random.normal(ks[3], (KVH * HD, D), jnp.float32) * s, 'Wv': jax.random.normal(ks[4], (KVH * HD, D), jnp.float32) * s, 'Wo': jax.random.normal(ks[5], (D, H * HD), jnp.float32) * s, 'q_norm_w': jnp.ones((HD,), jnp.float32), 'k_norm_w': jnp.ones((HD,), jnp.float32)}
    _L0_xattn_all = _L0_xattn_setup()
    _L0_xattn_in = {k: v for k, v in _L0_xattn_all.items() if k in ('Wq', 'Wk', 'Wv', 'Wo', 'q_norm_w', 'k_norm_w')}
    del _L0_xattn_all

    def _L0_ffn_setup():
        import jax, jax.numpy as jnp
        import numpy as np
        IN_F = 512
        OUT_F = 512
        RANK = 8
        NUM_EXPERTS = 64
        TOP_K = 16
        ROUTER_DIM = 16
        ALPHA = 32
        SCALING = ALPHA / TOP_K
        BOTTLENECK = NUM_EXPERTS * RANK
        key = jax.random.key(seed)
        ks = jax.random.split(key, 5)
        x = jax.random.normal(ks[0], (4, 512, IN_F), dtype=jnp.float32)
        bound_a = float(np.sqrt(6.0 / IN_F))
        A_w = jax.random.uniform(ks[1], (BOTTLENECK, IN_F), jnp.float32, -bound_a, bound_a)
        B_w = jax.random.normal(ks[2], (OUT_F, BOTTLENECK), dtype=jnp.float32) * 0.02
        Wq_w = jax.random.normal(ks[3], (ROUTER_DIM, IN_F), dtype=jnp.float32) * 0.02
        keys = jax.random.normal(ks[4], (NUM_EXPERTS, ROUTER_DIM), dtype=jnp.float32) * 0.01
        return {'x': x, 'A_w': A_w, 'B_w': B_w, 'Wq_w': Wq_w, 'keys': keys}
    _L0_ffn_all = _L0_ffn_setup()
    _L0_ffn_in = {k: v for k, v in _L0_ffn_all.items() if k in ('A_w', 'B_w', 'Wq_w', 'keys')}
    del _L0_ffn_all

    def _L1_xattn_setup():
        import jax, jax.numpy as jnp
        import numpy as np
        B, LQ, LK, D, H, DH = (2, 128, 128, 512, 32, 128)
        EPS = 1e-05

        def _rmsnorm(x, weight):
            var = jnp.mean(jnp.square(x), axis=-1, keepdims=True)
            return x * jax.lax.rsqrt(var + EPS) * weight
        key = jax.random.key(seed)
        ks = jax.random.split(key, 8)
        scale = 0.02
        return {'hidden_states': jax.random.normal(ks[0], (B, LQ, D), jnp.float32), 'key_value_states': jax.random.normal(ks[1], (B, LK, D), jnp.float32), 'attention_mask': jax.random.randint(ks[2], (B, LQ, LK), 0, 2) > 0, 'position_bias': jax.random.normal(ks[3], (H, LQ, LK), jnp.float32), 'ln_weight': jnp.ones((D,), jnp.float32), 'w_q': jax.random.normal(ks[4], (H * DH, D), jnp.float32) * scale, 'w_k': jax.random.normal(ks[5], (H * DH, D), jnp.float32) * scale, 'w_v': jax.random.normal(ks[6], (H * DH, D), jnp.float32) * scale, 'w_out': jax.random.normal(ks[7], (D, H * DH), jnp.float32) * scale}
    _L1_xattn_all = _L1_xattn_setup()
    _L1_xattn_in = {k: v for k, v in _L1_xattn_all.items() if k in ('position_bias', 'ln_weight', 'w_q', 'w_k', 'w_v', 'w_out')}
    del _L1_xattn_all

    def _L1_ffn_setup():
        import jax, jax.numpy as jnp
        import numpy as np
        GROUP = 64

        def dequant_q40(w, s, out_features, in_features):
            msb = w >> 4
            lsb = (w & 15 ^ 8) - 8
            g = jnp.concatenate([msb, lsb], axis=1).reshape(-1, GROUP)
            deq = g.astype(s.dtype) * s[:, None]
            return deq.reshape(out_features, in_features)
        key = jax.random.key(seed)
        ks = jax.random.split(key, 7)
        dim, hidden = (512, 1376)
        B, S = (2, 256)

        def packed(k, din, dout):
            return jax.random.randint(k, (din * dout // GROUP // 2, GROUP), -128, 128, dtype=jnp.int32)

        def scales(k, din, dout):
            return (jax.random.uniform(k, (din * dout // GROUP,), dtype=jnp.float32) + 0.5) * 0.01
        x = jax.random.normal(ks[0], (B, S, dim), dtype=jnp.float32)
        w1 = packed(ks[1], dim, hidden)
        s1 = scales(ks[2], dim, hidden)
        w2 = packed(ks[3], hidden, dim)
        s2 = scales(ks[4], hidden, dim)
        w3 = packed(ks[5], dim, hidden)
        s3 = scales(ks[6], dim, hidden)
        return {'x': x, 'w1': w1, 's1': s1, 'w2': w2, 's2': s2, 'w3': w3, 's3': s3}
    _L1_ffn_all = _L1_ffn_setup()
    _L1_ffn_in = {k: v for k, v in _L1_ffn_all.items() if k in ('w1', 's1', 'w2', 's2', 'w3', 's3')}
    del _L1_ffn_all
    return {'x': x, 'ctx_4096': ctx_4096, 'mask_1x1xSxS2_ff0': mask_1x1xSxS2_ff0, 'mask_BxSxS2_bk0': mask_BxSxS2_bk0, 'L0_xattn_Wq': _L0_xattn_in['Wq'], 'L0_xattn_Wk': _L0_xattn_in['Wk'], 'L0_xattn_Wv': _L0_xattn_in['Wv'], 'L0_xattn_Wo': _L0_xattn_in['Wo'], 'L0_xattn_q_norm_w': _L0_xattn_in['q_norm_w'], 'L0_xattn_k_norm_w': _L0_xattn_in['k_norm_w'], 'L0_ffn_A_w': _L0_ffn_in['A_w'], 'L0_ffn_B_w': _L0_ffn_in['B_w'], 'L0_ffn_Wq_w': _L0_ffn_in['Wq_w'], 'L0_ffn_keys': _L0_ffn_in['keys'], 'L1_xattn_position_bias': _L1_xattn_in['position_bias'], 'L1_xattn_ln_weight': _L1_xattn_in['ln_weight'], 'L1_xattn_w_q': _L1_xattn_in['w_q'], 'L1_xattn_w_k': _L1_xattn_in['w_k'], 'L1_xattn_w_v': _L1_xattn_in['w_v'], 'L1_xattn_w_out': _L1_xattn_in['w_out'], 'L1_ffn_w1': _L1_ffn_in['w1'], 'L1_ffn_s1': _L1_ffn_in['s1'], 'L1_ffn_w2': _L1_ffn_in['w2'], 'L1_ffn_s2': _L1_ffn_in['s2'], 'L1_ffn_w3': _L1_ffn_in['w3'], 'L1_ffn_s3': _L1_ffn_in['s3']}

def reference(x, ctx_4096, mask_1x1xSxS2_ff0, mask_BxSxS2_bk0, L0_xattn_Wq, L0_xattn_Wk, L0_xattn_Wv, L0_xattn_Wo, L0_xattn_q_norm_w, L0_xattn_k_norm_w, L0_ffn_A_w, L0_ffn_B_w, L0_ffn_Wq_w, L0_ffn_keys, L1_xattn_position_bias, L1_xattn_ln_weight, L1_xattn_w_q, L1_xattn_w_k, L1_xattn_w_v, L1_xattn_w_out, L1_ffn_w1, L1_ffn_s1, L1_ffn_w2, L1_ffn_s2, L1_ffn_w3, L1_ffn_s3):
    import jax
    import jax.numpy as jnp

    def _L0_xattn_ref(hidden_states, cross_attention_states, attention_mask, Wq, Wk, Wv, Wo, q_norm_w, k_norm_w):
        import jax, jax.numpy as jnp
        import numpy as np
        B, Q, K, D = (1, 128, 6404, 512)
        H, KVH, HD = (32, 8, 128)
        GROUPS = H // KVH
        EPS = 1e-05

        def _rmsnorm(x, w):
            xf = x.astype(jnp.float32)
            var = jnp.mean(xf * xf, axis=-1, keepdims=True)
            return (xf * jax.lax.rsqrt(var + EPS)).astype(x.dtype) * w
        bsz, q_len, _ = hidden_states.shape
        kv_len = cross_attention_states.shape[1]
        q = (hidden_states @ Wq.T).reshape(bsz, q_len, H, HD).transpose(0, 2, 1, 3)
        k = (cross_attention_states @ Wk.T).reshape(bsz, kv_len, KVH, HD).transpose(0, 2, 1, 3)
        v = (cross_attention_states @ Wv.T).reshape(bsz, kv_len, KVH, HD).transpose(0, 2, 1, 3)
        q = _rmsnorm(q, q_norm_w)
        k = jnp.repeat(k, GROUPS, axis=1)
        v = jnp.repeat(v, GROUPS, axis=1)
        k = _rmsnorm(k, k_norm_w)
        scale = 1.0 / np.sqrt(HD)
        scores = jnp.einsum('bhqd,bhkd->bhqk', q, k) * scale
        scores = scores + attention_mask[:, :, :, :kv_len]
        probs = jax.nn.softmax(scores.astype(jnp.float32), axis=-1).astype(q.dtype)
        out = jnp.einsum('bhqk,bhkd->bhqd', probs, v)
        out = out.transpose(0, 2, 1, 3).reshape(bsz, q_len, H * HD)
        return out @ Wo.T

    def _L0_ffn_ref(x, A_w, B_w, Wq_w, keys):
        import jax, jax.numpy as jnp
        import numpy as np
        IN_F = 512
        OUT_F = 512
        RANK = 8
        NUM_EXPERTS = 64
        TOP_K = 16
        ROUTER_DIM = 16
        ALPHA = 32
        SCALING = ALPHA / TOP_K
        BOTTLENECK = NUM_EXPERTS * RANK
        q = jnp.einsum('bsd,rd->bsr', x, Wq_w)
        scores = jnp.einsum('bsr,er->bse', q, keys)
        top_vals, top_idx = jax.lax.top_k(scores, TOP_K)
        top_w = jax.nn.softmax(top_vals, axis=-1)
        gate = jnp.sum(jax.nn.one_hot(top_idx, NUM_EXPERTS, dtype=top_w.dtype) * top_w[..., None], axis=-2)
        z = jnp.einsum('bsd,nd->bsn', x, A_w)
        z = z.reshape(*z.shape[:-1], NUM_EXPERTS, RANK)
        z_gated = (z * gate[..., None]).reshape(*z.shape[:-2], BOTTLENECK)
        out = jnp.einsum('bsn,on->bso', z_gated, B_w) * SCALING
        return out

    def _L1_xattn_ref(hidden_states, key_value_states, attention_mask, position_bias, ln_weight, w_q, w_k, w_v, w_out):
        import jax, jax.numpy as jnp
        import numpy as np
        B, LQ, LK, D, H, DH = (2, 128, 128, 512, 32, 128)
        EPS = 1e-05

        def _rmsnorm(x, weight):
            var = jnp.mean(jnp.square(x), axis=-1, keepdims=True)
            return x * jax.lax.rsqrt(var + EPS) * weight
        x = _rmsnorm(hidden_states, ln_weight)
        b, lq, _ = x.shape
        lk = key_value_states.shape[1]
        h_q = (x @ w_q.T).reshape(b, lq, H, DH)
        h_k = (key_value_states @ w_k.T).reshape(b, lk, H, DH)
        h_v = (key_value_states @ w_v.T).reshape(b, lk, H, DH)
        score = jnp.einsum('bqhd,bkhd->bhqk', h_q, h_k)
        score = score + position_bias[None]
        m = attention_mask[:, None]
        score = jnp.where(m, score, -jnp.inf)
        score = jax.nn.softmax(score, axis=-1)
        score = jnp.where(m, score, 0.0)
        attn = jnp.einsum('bhqk,bkhd->bqhd', score, h_v).reshape(b, lq, H * DH)
        out = attn @ w_out.T
        return hidden_states + out

    def _L1_ffn_ref(x, w1, s1, w2, s2, w3, s3):
        import jax, jax.numpy as jnp
        import numpy as np
        GROUP = 64

        def dequant_q40(w, s, out_features, in_features):
            msb = w >> 4
            lsb = (w & 15 ^ 8) - 8
            g = jnp.concatenate([msb, lsb], axis=1).reshape(-1, GROUP)
            deq = g.astype(s.dtype) * s[:, None]
            return deq.reshape(out_features, in_features)
        dim = x.shape[-1]
        hidden = w1.shape[0] * w1.shape[1] * 2 // dim
        W1 = dequant_q40(w1, s1, hidden, dim)
        W3 = dequant_q40(w3, s3, hidden, dim)
        W2 = dequant_q40(w2, s2, dim, hidden)
        a = jnp.einsum('bsd,hd->bsh', x, W1)
        b = jnp.einsum('bsd,hd->bsh', x, W3)
        h = jax.nn.silu(a) * b
        return jnp.einsum('bsh,dh->bsd', h, W2)
    x = x + _L0_xattn_ref(_layernorm(x, axis=-1), ctx_4096, mask_1x1xSxS2_ff0, L0_xattn_Wq, L0_xattn_Wk, L0_xattn_Wv, L0_xattn_Wo, L0_xattn_q_norm_w, L0_xattn_k_norm_w)
    x = x + _L0_ffn_ref(_layernorm(x, axis=-1), L0_ffn_A_w, L0_ffn_B_w, L0_ffn_Wq_w, L0_ffn_keys)
    x = x + _L1_xattn_ref(_layernorm(x, axis=-1), ctx_4096, mask_BxSxS2_bk0, L1_xattn_position_bias, L1_xattn_ln_weight, L1_xattn_w_q, L1_xattn_w_k, L1_xattn_w_v, L1_xattn_w_out)
    x = x + _L1_ffn_ref(_layernorm(x, axis=-1), L1_ffn_w1, L1_ffn_s1, L1_ffn_w2, L1_ffn_s2, L1_ffn_w3, L1_ffn_s3)
    return x

_drawn_inputs = setup_inputs


def setup_inputs(seed=0):
    import zlib

    import numpy as np

    out = dict(_drawn_inputs(seed))
    spreads = {'L0_xattn_q_norm_w': (1.0, 0.58),
     'L0_xattn_k_norm_w': (1.0, 0.6),
     'L1_xattn_ln_weight': (1.0, 0.2)}
    factors = {}
    for name, (base, spread) in spreads.items():
        noise = np.random.default_rng([zlib.crc32(name.encode()), seed]).standard_normal(out[name].shape)
        drawn = base * np.exp(spread * noise) if base else spread * noise
        out[name] = jnp.asarray(drawn.astype(out[name].dtype))
    for name, factor in factors.items():
        out[name] = (out[name] * factor).astype(out[name].dtype)
    return out
```

```python
from contextlib import ExitStack

import concourse.bass as bass
from concourse import mybir

F32 = mybir.dt.float32
F32R = mybir.dt.float32r
I32 = mybir.dt.int32
U8 = mybir.dt.uint8
ALU = mybir.AluOpType
ACT = mybir.ActivationFunctionType
AX = mybir.AxisListType

P = 128
D = 512
KT = D // P
NB = 8
TOK = NB * P
HALF = TOK // 2
H = 32
KVH = 8
GH = H // KVH
GROUPS = H // GH
NE, RANK, RD = 64, 8, 16
HID = 1376
HT = -(-HID // P)
EPS = 1e-5
MASKED = -3.0e38
MAX_FLOOR = -1.0e37
RAW = 4


class Chunks:

    def __init__(self, before, pattern, times=1):
        self.pattern, self.times = pattern, times
        self.c0, self.p0, self.d0 = (before.c1, before.p1, before.d1) if before else (0, 0, 0)
        self.n, self.np, self.nd = len(pattern), pattern.count("P"), pattern.count("D")
        self.c1 = self.c0 + self.n * times
        self.p1 = self.p0 + self.np * times
        self.d1 = self.d0 + self.nd * times

    def slot(self, i):
        return (self.c0 + i) % RAW

    def loaded(self, t, i):
        return (t * (self.n // RAW) + (self.c0 + i) // RAW + 1) * 16

    def high(self, t, i):
        return t * self.n + (self.c0 + i + 1)

    def low(self, t, i):
        kind = self.pattern[i]
        done = self.pattern[: i + 1].count(kind)
        if kind == "P":
            return "P", t * self.np + (self.p0 + done)
        return "D", t * self.nd + (self.d0 + done)


def two_layer_block(
    nc, x_in, mask0, mask1, ctx_t, l0_q, l0_k, l0_v, l0_o, q_norm, k_norm, f0_a, f0_b, f0_r, f0_keys,
    bias, ln_w, l1_q, l1_k, l1_v, l1_o, f1_p1, f1_s1, f1_p3, f1_s3, f1_p2, f1_s2, shift_l, shift_r, out,
):
    kv_c = Chunks(None, "DPDPDPDP" "DPDP" "PPPPPPPPPPPP")
    q0_c = Chunks(kv_c, "PDPD")
    l0_c = Chunks(q0_c, "PPDDDPPP", GROUPS - 1)
    l0e_c = Chunks(l0_c, "PDDD")
    F0_R, F0_A, F0_B, F0_K, F0_V, F0_X, F0_Q, F0_Y, F0_Q1, F0_K1, F0_N = 0, 1, 5, 9, 10, 14, 18, 19, 23, 24, 25
    f0_c = Chunks(l0e_c, "P" * F0_N)
    l1_c = Chunks(f0_c, "PPPP" * GH, GROUPS - 1)
    l1e_c = Chunks(l1_c, "PPP" "PPP" "P" "P")
    L1E = {(0, "o"): 0, (0, "q"): 1, (0, "k"): 2, (1, "o"): 3, (1, "q"): 4, (1, "k"): 5, (2, "o"): 6, (3, "o"): 7}

    with ExitStack() as top:
        def alloc(stack, name, shape, dt=F32):
            return stack.enter_context(nc.sbuf_tensor(name, shape, dt))

        def sem(name):
            return top.enter_context(nc.semaphore(name))

        x = alloc(top, "x", [P, NB, D])
        xn_t = alloc(top, "xn_t", [P, 2, KT, TOK], F32R)
        wide = alloc(top, "wide", [P, 2, KT, TOK], F32R)
        raw = alloc(top, "raw", [P, RAW, D])
        ident = alloc(top, "ident", [P, P])
        m0 = alloc(top, "m0", [P, P])
        m1u = alloc(top, "m1u", [P, NB, P], U8)
        w_r = alloc(top, "w_r", [P, 2, D], F32R)
        keys = alloc(top, "keys", [RD, NE])
        qn_w = alloc(top, "qn_w", [P, 1])
        kn_w = alloc(top, "kn_w", [P, 1])
        qk_w = alloc(top, "qk_w", [P, 1])
        minus_half = alloc(top, "minus_half", [P, NB])
        st = alloc(top, "st", [P, NB, 6])
        mv = alloc(top, "mv", [P, NB, 2])
        xn = alloc(top, "xn", [P, 2, D])
        ve = alloc(top, "ve", [P, NB])
        ve2 = alloc(top, "ve2", [P, NB])
        rs = alloc(top, "rs", [P, NB])
        nmr = alloc(top, "nmr", [P, NB])
        hs = alloc(top, "hs", [P, NB])
        rr = alloc(top, "rr", [P, NB])
        shl = alloc(top, "shl", [P, 4], I32)
        shr = alloc(top, "shr", [P, 4], I32)
        sc0 = alloc(top, "sc0", [P, 8, GH])

        with ExitStack() as s:
            v0 = alloc(s, "v0", [P, NB, KVH * P])
            k_t = alloc(s, "k_t", [P, KVH * TOK])
            w_o0 = alloc(s, "w_o0", [P, 2, GH, D], F32R)
            with ExitStack() as s2:
                kv_w1 = alloc(s2, "kv_w1", [P, 2, KT, D], F32R)
                k_raw = alloc(s2, "k_raw", [P, 4, D])
                k_sq = alloc(s2, "k_sq", [P, D])
            with ExitStack() as s2:
                q_raw = alloc(s2, "q_raw", [P, 2, D])
                q_sq = alloc(s2, "q_sq", [P, D])
                q_t = alloc(s2, "q_t", [P, D])
                sm0 = alloc(s2, "sm0", [P, GH, P])
                p0 = alloc(s2, "p0", [P, GH, P])
                p_t0 = alloc(s2, "p_t0", [P, D])
                o_t0 = alloc(s2, "o_t0", [P, 2, 2, D], F32R)
                v_st = alloc(s2, "v_st", [P, 2, P])
        with ExitStack() as s:
            w_q1 = alloc(s, "w_q1", [P, 2, 2, D], F32R)
            w_k1 = alloc(s, "w_k1", [P, 2, 2, D], F32R)
            w_v1 = alloc(s, "w_v1", [P, 2, KT, D], F32R)
            w_o1 = alloc(s, "w_o1", [P, 2, 2, D], F32R)
            k_t1 = alloc(s, "k_t1", [P, 2, TOK])
            v1 = alloc(s, "v1", [P, NB, D])
            with ExitStack() as s2:
                z = alloc(s2, "z", [P, NB, D])
                z_t = alloc(s2, "z_t", [P, 2, 2, D], F32R)
                qr = alloc(s2, "qr", [RD, TOK])
                scr = alloc(s2, "scr", [P, NB, NE])
                top1 = alloc(s2, "top1", [P, NB, 8])
                top2 = alloc(s2, "top2", [P, NB, 8])
                rep1 = alloc(s2, "rep1", [P, NB, NE])
                rep2 = alloc(s2, "rep2", [P, NB, NE])
                gate = alloc(s2, "gate", [P, NB, NE])
                gsum = alloc(s2, "gsum", [P, NB])
                ginv = alloc(s2, "ginv", [P, NB])
                xw2 = alloc(s2, "xw2", [P, 2, D])
                lnw = alloc(s2, "lnw", [P, D])
            with ExitStack() as s2:
                m1 = alloc(s2, "m1", [P, NB, P])
                q_t1 = alloc(s2, "q_t1", [P, 2, TOK])
                sm1 = alloc(s2, "sm1", [P, 2, 4, P])
                p1 = alloc(s2, "p1", [P, 2, 4, P])
                p_t1 = alloc(s2, "p_t1", [P, 2, D])
                o_t1 = alloc(s2, "o_t1", [P, 2, 2, TOK], F32R)
                b_sb = alloc(s2, "b_sb", [P, 2, P])
                nmx1 = alloc(s2, "nmx1", [P, 2, 4])
                sum1 = alloc(s2, "sum1", [P, 2, 4])
                inv1 = alloc(s2, "inv1", [P, 2, 4])
        with ExitStack() as s:
            pk = alloc(s, "pk", [P, 3, D], I32)
            ps = alloc(s, "ps", [P, 3, D])
            sh = alloc(s, "sh", [P, 3, D], I32)
            dq = alloc(s, "dq", [P, 3, D])
            w_g = alloc(s, "w_g", [P, 2, 2, D], F32R)
            w_u = alloc(s, "w_u", [P, 2, 2, D], F32R)
            w_d = alloc(s, "w_d", [P, 2, 2, D], F32R)
            h_t = alloc(s, "h_t", [P, 2, 2, TOK], F32R)
            sl = alloc(s, "sl", [P, 2, HALF])
            hf = alloc(s, "hf", [P, 2, HALF])
        bank = top.enter_context(nc.psum_tensor("bank", [P, 8, 512], F32))

        raw_loaded = [sem(f"raw_loaded{i}") for i in range(RAW)]
        w_high, w_low_p, w_low_d = sem("w_high"), sem("w_low_pool"), sem("w_low_vector")
        x_loaded, small_loaded, keys_loaded, lnw_loaded = sem("x_loaded"), sem("small_loaded"), sem("keys_loaded"), sem("lnw_loaded")
        ones_set, ident_set, qk_w_set, mask_set = sem("ones_set"), sem("ident_set"), sem("qk_w_set"), sem("mask_set")
        kv_mm, kv_out, k_squared, k_sum, k_eps, k_rstd, k_hat, kt_mm, kt_out = (
            sem(n) for n in ("kv_mm", "kv_out", "k_squared", "k_sum", "k_eps", "k_rstd", "k_hat", "kt_mm", "kt_out"))
        ln_sems = [{n: sem(f"ln{i}_{n}") for n in ("stats", "aggr", "eps", "rstd", "nmr", "xn", "tr", "high", "low")} for i in range(4)]
        ln2_ss, ln2_eps, ln2_rr, ln2_res, ln2_w = (sem("ln2_" + n) for n in ("ss", "e2", "rr", "res", "w"))
        (q_mm, q_out, q_squared, q_sum, q_eps, q_rstd, q_hat, qt_mm, qt_out, s_mm, s_masked, s_max, p_exp, p_inv, p_norm,
         pt_mm, pt_out, v_staged, pv_mm, ot_high, ot_low, o_mm, x_added) = (
            sem("a0_" + n) for n in (
                "q_mm", "q_out", "q_squared", "q_sum", "q_eps", "q_rstd", "q_hat", "qt_mm", "qt_out", "s_mm", "s_masked",
                "s_max", "p_exp", "p_inv", "p_norm", "pt_mm", "pt_out", "v_staged", "pv_mm", "ot_high", "ot_low", "o_mm", "x_added"))
        (r_mm, r_out, sc_mm, sc_out, t1_done, rep1_done, t2_done, rep2_done, sel_done, sub_done, exp_done, gated, g_sum, g_inv,
         g_done, z_mm, z_out, z_gated, zt_mm, zt_high, zt_low, f0_mm, f0_added) = (
            sem("f0_" + n) for n in (
                "r_mm", "r_out", "sc_mm", "sc_out", "t1", "rep1", "t2", "rep2", "sel", "sub", "exp", "gated", "sum", "inv",
                "gate", "z_mm", "z_out", "z_gated", "zt_mm", "zt_high", "zt_low", "mm", "added"))
        (q1_mm, k1_mm, q1_out, k1_out, v1_mm, v1_out, s1_mm, s1_biased, s1_masked, s1_max, s1_floor, p1_exp, p1_guard, p1_inv, p1_norm, pt1_mm, pt1_out,
         pv1_mm, ot1_high, ot1_low, o1_mm, x1_added) = (
            sem("a1_" + n) for n in (
                "q_mm", "k_mm", "q_out", "k_out", "v_mm", "v_out", "s_mm", "s_biased", "s_masked", "s_max", "s_floor", "p_exp", "p_guard", "p_inv", "p_norm",
                "pt_mm", "pt_out", "pv_mm", "ot_high", "ot_low", "o_mm", "x_added"))
        bias_loaded = [sem(f"bias_loaded{i}") for i in range(2)]
        pk_loaded = [sem(f"packed_loaded{i}") for i in range(3)]
        unpacked, scaled, f1_high, f1_low, ab_mm, silu_done, h_done, h_high, h_low, f1_mm, f1_added = (
            sem("f1_" + n) for n in ("unpacked", "scaled", "high", "low", "ab_mm", "silu", "h", "h_high", "h_low", "mm", "added"))
        stored = sem("stored")

        block = top.enter_context(nc.Block())

        def wait_low(eng, chunks, t, i):
            kind, n = chunks.low(t, i)
            eng.wait_ge(w_low_p if kind == "P" else w_low_d, n)

        def wait_lows(eng, chunks, t, first, last):
            for kind in "PD":
                own = [i for i in range(first, last + 1) if chunks.pattern[i] == kind]
                if own:
                    wait_low(eng, chunks, t, own[-1])

        def load(sp, chunks, t, i, src):
            r = i - RAW
            if isinstance(t, int) and chunks.c0 + t * chunks.n + r < 0:
                pass
            elif r >= 0:
                wait_low(sp, chunks, t, r)
            else:
                before, tb, ib = owner(chunks, t, r)
                wait_low(sp, before, tb, ib)
            sp.dma_start(raw[:, chunks.slot(i), :], src).then_inc(raw_loaded[chunks.slot(i)], 16)

        order = [kv_c, q0_c, l0_c, l0e_c, f0_c, l1_c, l1e_c]

        def owner(chunks, t, r):
            if not isinstance(t, int) or t > 0:
                assert -r <= chunks.n
                return chunks, t - 1, chunks.n + r
            k = order.index(chunks) - 1
            while -r > order[k].n * order[k].times:
                r += order[k].n * order[k].times
                k -= 1
            b = order[k]
            at = b.n * b.times + r
            return b, at // b.n, at % b.n

        def high(act, chunks, t, i, dst):
            act.wait_ge(raw_loaded[chunks.slot(i)], chunks.loaded(t, i))
            act.activation(dst, raw[:, chunks.slot(i), :], ACT.Copy).then_inc(w_high, 1)

        def low(eng, chunks, t, i, dst, dst_high):
            eng.wait_ge(w_high, chunks.high(t, i))
            eng.tensor_tensor(dst, raw[:, chunks.slot(i), :], dst_high.bitcast(F32), ALU.subtract).then_inc(
                w_low_p if chunks.pattern[i] == "P" else w_low_d, 1)

        def product(pe, dst, terms, first=True, final=True, before=None):
            n = len(terms)
            for k, ((lh, ll), (rh, rl)) in enumerate(terms):
                if before:
                    before(k)
                pe.matmul(dst, lh, rh, start=(first and k == 0), stop=False)
                pe.matmul(dst, lh, rl, start=False, stop=False)
                last = pe.matmul(dst, ll, rh, start=False, stop=(final and k == n - 1))
            return last

        def xn_tile(b):
            return [(xn_t[:, 0, kt, b * P:(b + 1) * P], xn_t[:, 1, kt, b * P:(b + 1) * P]) for kt in range(KT)]

        def xn_half(f):
            return [(xn_t[:, 0, kt, f * HALF:(f + 1) * HALF], xn_t[:, 1, kt, f * HALF:(f + 1) * HALF]) for kt in range(KT)]

        def ctx_tile(b):
            return [(wide[:, 0, kt, b * P:(b + 1) * P], wide[:, 1, kt, b * P:(b + 1) * P]) for kt in range(KT)]

        def heads4(ap):
            return ap.rearrange("p (h n) -> p h n", h=GH)

        def over(ap, n):
            return ap.unsqueeze(2).broadcast_to([P, ap.shape[1], n])

        def repeat(ap, n):
            return ap.unsqueeze(1).broadcast_to([P, n, ap.shape[1]])

        def transposes(pe, dst, src):
            for k in range(4):
                last = pe.transpose(bank[:, dst, k * P:(k + 1) * P], src[:, k * P:(k + 1) * P], ident[:, :])
            return last

        LN_BANKS = ((4, 5), (6, 7), (2, 3), (2, 3))

        def ln_stats(dve, i, b):
            L = ln_sems[i]
            dve.bn_stats(st[:, b, :], x[:, b, :]).then_inc(L["stats"], 1)
            dve.wait_ge(L["stats"], b + 1)
            dve.bn_aggr(mv[:, b, :], st[:, b, :]).then_inc(L["aggr"], 1)
            if b % 4 == 3:
                dve.wait_ge(L["aggr"], b + 1)
                dve.tensor_scalar(ve[:, b - 3:b + 1], mv[:, b - 3:b + 1, 1], EPS, None, ALU.add).then_inc(L["eps"], 1)

        def ln_rstd(pool, i, f):
            L = ln_sems[i]
            pool.wait_ge(L["eps"], f + 1)
            pool.tensor_tensor(rs[:, 4 * f:4 * f + 4], ve[:, 4 * f:4 * f + 4], minus_half[:, 0:4], ALU.pow).then_inc(L["rstd"], 1)

        def ln_nmr(dve, i, f):
            L = ln_sems[i]
            dve.wait_ge(L["rstd"], f + 1)
            dve.scalar_tensor_tensor(nmr[:, 4 * f:4 * f + 4], mv[:, 4 * f:4 * f + 4, 0], -1.0, rs[:, 4 * f:4 * f + 4],
                                     ALU.mult, ALU.mult).then_inc(L["nmr"], 1)

        def ln_apply(act, i, b):
            L = ln_sems[i]
            act.wait_ge(L["nmr"], b // 4 + 1)
            if b >= 2:
                act.wait_ge(L["tr"], b - 1)
            act.activation(xn[:, b % 2, :], x[:, b, :], ACT.Identity, bias=nmr[:, b:b + 1], scale=rs[:, b:b + 1]).then_inc(L["xn"], 1)

        def ln_transpose(pe, i, b, src=None, ready=None):
            L = ln_sems[i]
            pe.wait_ge(ready or L["xn"], b + 1)
            if b >= 2:
                pe.wait_ge(L["low"], b - 1)
            transposes(pe, LN_BANKS[i][b % 2], (src or xn)[:, b % 2, :]).then_inc(L["tr"], 1)

        def ln_high(act, i, b):
            L = ln_sems[i]
            act.wait_ge(L["tr"], b + 1)
            act.activation(xn_t[:, 0, :, b * P:(b + 1) * P], heads4(bank[:, LN_BANKS[i][b % 2], :]), ACT.Copy).then_inc(L["high"], 1)

        def ln_low(dve, i, b):
            L = ln_sems[i]
            dve.wait_ge(L["high"], b + 1)
            dve.tensor_tensor(xn_t[:, 1, :, b * P:(b + 1) * P], heads4(bank[:, LN_BANKS[i][b % 2], :]),
                              xn_t[:, 0, :, b * P:(b + 1) * P].bitcast(F32), ALU.subtract).then_inc(L["low"], 1)

        def kv_slot(m, part, kt):
            return (w_o0 if m % 2 == 0 else kv_w1)[:, part, kt, :]

        def kv_what(i):
            if i < 8:
                return ("ctx", 0, i // 2) if i % 2 == 0 else ("w", 0, i // 2)
            return ("ctx", 1, i - 8) if i < 12 else ("w", 1 + (i - 12) // 4, i % 4)

        def kv_dst(i, part):
            what, m, kt = kv_what(i)
            return wide[:, part, kt, m * HALF:(m + 1) * HALF] if what == "ctx" else kv_slot(m, part, kt)

        def kv_src(i):
            what, m, kt = kv_what(i)
            return ctx_t[m, kt] if what == "ctx" else (l0_k if m < 2 else l0_v)[m % 2, kt]

        def kv_free(eng, i):
            if i == 16:
                eng.wait_ge(kv_mm, 8)
            if i == 20:
                eng.wait_ge(kv_mm, 16)

        def wq_slot(par, part, kt):
            if isinstance(par, int):
                return wide[:, part, kt, par * D:(par + 1) * D]
            return wide[:, part, kt, bass.ds(par * D, D)]

        L0_ITEMS = [("q", 0, 0), ("o", 0, 1), ("o", 1, 1), ("o", 2, 2), ("o", 3, 2), ("q", 1, 3), ("q", 2, 4), ("q", 3, 5)]

        def l0_items(g, b, last):
            if last:
                return [(l0e_c, 0, k, "o", k) for k, bb in enumerate((1, 1, 2, 2)) if bb == b]
            return [(l0_c, g, k, what, piece) for k, (what, piece, bb) in enumerate(L0_ITEMS) if bb == b]

        def l0_dst(g, what, piece, part):
            return w_o0[:, part, piece, :] if what == "o" else wq_slot((g + 1) % 2, part, piece)

        def l0_free(eng, g, b, what, piece):
            first = isinstance(g, int) and g == 0
            if what == "o" and piece == 0:
                if first:
                    eng.wait_ge(kv_mm, 32)
                else:
                    eng.wait_ge(o_mm, 8 * g)

        def f0_dst(i, part):
            if i == F0_R:
                return w_r[:, part, :]
            if i < F0_B:
                return wide[:, part, i - F0_A, 0:D]
            if i < F0_K:
                return wide[:, part, i - F0_B, D:2 * D]
            if F0_V <= i < F0_X:
                return w_v1[:, part, i - F0_V, :]
            if F0_X <= i < F0_Q:
                return wide[:, part, i - F0_X, 0:HALF]
            if F0_Y <= i < F0_Q1:
                return wide[:, part, i - F0_Y, HALF:TOK]
            w, head = {F0_K: (w_k1, 0), F0_Q: (w_q1, 0), F0_Q1: (w_q1, 1), F0_K1: (w_k1, 1)}[i]
            return w[:, head, part, :]

        def f0_src(i):
            if i == F0_R:
                return f0_r
            if i < F0_B:
                return f0_a[0, i - F0_A]
            if i < F0_K:
                return f0_b[0, i - F0_B]
            if F0_V <= i < F0_X:
                return l1_v[0, i - F0_V]
            if F0_X <= i < F0_Q:
                return ctx_t[0, i - F0_X]
            if F0_Y <= i < F0_Q1:
                return ctx_t[1, i - F0_Y]
            return {F0_K: l1_k[0], F0_Q: l1_q[0], F0_Q1: l1_q[1], F0_K1: l1_k[1]}[i]

        def f0_free(eng, i):
            if i == F0_A:
                eng.wait_ge(q_mm, 56)
            if i == F0_B:
                eng.wait_ge(q_mm, 64)
            if i == F0_K:
                eng.wait_ge(o_mm, 64)
            if i == F0_X:
                eng.wait_ge(z_mm, NB)
            if i == F0_Y:
                eng.wait_ge(f0_mm, NB)

        F0_EARLY = {3: (F0_R, F0_A), 4: (F0_A + 1, F0_A + 2), 5: (F0_A + 3,), 6: (F0_B, F0_B + 1), 7: (F0_B + 2, F0_B + 3)}

        def l1_items(g, j, last):
            if last:
                return [(l1e_c, 0, L1E[(j, w)], w) for w in "oqk" if (j, w) in L1E]
            return [(l1_c, g, 4 * j + k, w) for k, w in enumerate("oqkv")]

        def l1_dst(j, what, part):
            if what == "q":
                return w_q1[:, j % 2, part, :]
            if what == "k":
                return w_k1[:, j % 2, part, :]
            if what == "o":
                return w_o1[:, j % 2, part, :]
            return w_v1[:, part, j, :]

        def l1_src(g, j, what):
            n = 4 * g + j
            if what == "v":
                return l1_v[bass.ds(g + 1, 1), j].rearrange("a p n -> (a p) n")
            w, k = {"q": (l1_q, n + 2), "k": (l1_k, n + 2), "o": (l1_o, n)}[what]
            return w[k] if isinstance(k, int) else w[bass.ds(k, 1)].rearrange("a p n -> (a p) n")

        def l1_free(eng, g, j, what):
            if what == "q":
                eng.wait_ge(k1_mm, 8 * g + 2 * j + 2)
            if what == "o" and not (isinstance(g, int) and g == 0 and j < 2):
                eng.wait_ge(o1_mm, 16 * g + 8 * (j // 2))
            if what == "v" and j == 0:
                eng.wait_ge(v1_mm, 8 * g + 8)

        def groups(eng, body):
            body(0, True, False)
            with eng.Fori(1, GROUPS - 1) as g:
                body(g, False, False)
            body(GROUPS - 1, False, True)

        @block.sync
        def _(sp):
            for i in range(kv_c.n):
                load(sp, kv_c, 0, i, kv_src(i))
                if i == 11:
                    for b in range(NB):
                        sp.dma_start(x[:, b, :], x_in[b]).then_inc(x_loaded, 16)
            for i in range(4):
                load(sp, q0_c, 0, i, l0_q[0, i])

            def group(g, first, last):
                for b in range(NB):
                    for chunks, t, i, what, piece in l0_items(g, b, last):
                        if what == "o":
                            h = GH * g + piece
                            src = l0_o[h] if isinstance(h, int) else l0_o[bass.ds(h, 1)].rearrange("a p n -> (a p) n")
                        else:
                            src = l0_q[g + 1, piece] if isinstance(g, int) else l0_q[bass.ds(g + 1, 1), piece].rearrange("a p n -> (a p) n")
                        load(sp, chunks, t, i, src)
            groups(sp, group)
            for i in range(f0_c.n):
                load(sp, f0_c, 0, i, f0_src(i))
                if i == F0_K:
                    sp.wait_ge(o_mm, 64)
                    sp.dma_start(lnw[:, :], ln_w.partition_broadcast(P)).then_inc(lnw_loaded, 16)
            sp.wait_ge(ln_sems[2]["tr"], NB)
            for h in range(2):
                sp.dma_start(b_sb[:, h, :], bias[h]).then_inc(bias_loaded[h], 16)

            def group1(g, first, last):
                for j in range(GH):
                    for chunks, t, i, what in l1_items(g, j, last):
                        load(sp, chunks, t, i, l1_src(g, j, what))
                    if not (last and j >= 2):
                        n = 4 * g + j
                        src = bias[n + 2] if isinstance(n, int) else bias[bass.ds(n + 2, 1)].rearrange("a p n -> (a p) n")
                        sp.wait_ge(s1_biased, 2 * n + 2)
                        sp.dma_start(b_sb[:, j % 2, :], src).then_inc(bias_loaded[j % 2], 16)
            groups(sp, group1)
            sp.wait_ge(k1_mm, 2 * H)
            sp.wait_ge(v1_mm, NB * GROUPS)
            for t in range(HT):
                for k, (p, s_) in enumerate(((f1_p1, f1_s1), (f1_p3, f1_s3), (f1_p2, f1_s2))):
                    if t >= 1:
                        sp.wait_ge(scaled, 3 * (t - 1) + k + 1)
                    sp.dma_start(pk[:, k, :], p[t]).then_inc(pk_loaded[k], 16)
                    sp.dma_start(ps[:, k, :], s_[t]).then_inc(pk_loaded[k], 16)
            for b in range(NB):
                sp.wait_ge(f1_added, NB * (HT - 1) + b + 1)
                sp.dma_start(out[b], x[:, b, :]).then_inc(stored, 16)
            sp.wait_ge(stored, 16 * NB)

        @block.gpsimd
        def _(pool):
            pool.memset(minus_half[:, :], -0.5).then_inc(ones_set, 1)
            pool.memset(ident[:, :], 0.0).then_inc(ident_set, 1)
            pool.wait_ge(ident_set, 1)
            pool.affine_select(out=ident[:, :], in_=ident[:, :], compare_op=ALU.not_equal, fill=1.0, base=0,
                               pattern=[[-1, P]], channel_multiplier=1).then_inc(ident_set, 1)
            pool.wait_ge(ones_set, 1)

            at = {0: range(0, 12), 1: range(12, 16), 9: range(16, 20), 17: range(20, 24)}
            for i in range(24):
                for c in at.get(i, ()):
                    if kv_c.pattern[c] == "P":
                        low(pool, kv_c, 0, c, kv_dst(c, 1), kv_dst(c, 0))
                if i < 16:
                    pool.wait_ge(k_eps, i + 1)
                    if i >= 1:
                        pool.wait_ge(k_hat, i)
                    pool.tensor_tensor(sc0[:, 2, :], sc0[:, 1, :], minus_half[:, 0:GH], ALU.pow).then_inc(k_rstd, 1)
                if i == 16:
                    ln_rstd(pool, 0, 0)
                    ln_rstd(pool, 0, 1)
            for c in range(4):
                if q0_c.pattern[c] == "P":
                    low(pool, q0_c, 0, c, wq_slot(0, 1, c), wq_slot(0, 0, c))

            def square(s, b):
                pool.wait_ge(q_out, s + 1)
                if not (isinstance(s, int) and s == 0):
                    pool.wait_ge(q_sum, s)
                pool.tensor_tensor(q_sq[:, :], q_raw[:, b % 2, :], q_raw[:, b % 2, :], ALU.mult).then_inc(q_squared, 1)

            def normalise(s, b):
                pool.wait_ge(q_eps, s + 1)
                if not (isinstance(s, int) and s == 0):
                    pool.wait_ge(q_hat, s)
                pool.tensor_tensor(sc0[:, 4, :], sc0[:, 3, :], minus_half[:, 0:GH], ALU.pow).then_inc(q_rstd, 1)
                pool.wait_ge(q_rstd, s + 1)
                q = heads4(q_raw[:, b % 2, :])
                pool.tensor_tensor(q, q, over(sc0[:, 4, :], P), ALU.mult).then_inc(q_hat, 1)

            square(0, 0)
            normalise(0, 0)
            square(1, 1)

            def group(g, first, last):
                for b in range(NB):
                    s = NB * g + b
                    if not (last and b == 7):
                        normalise(s + 1, b + 1)
                    if not (last and b >= 6):
                        square(s + 2, b)
                    for chunks, t, i, what, piece in l0_items(g, b, last):
                        if chunks.pattern[i] == "P":
                            low(pool, chunks, t, i, l0_dst(g, what, piece, 1), l0_dst(g, what, piece, 0))
                    if last:
                        for i in F0_EARLY.get(b, ()):
                            low(pool, f0_c, 0, i, f0_dst(i, 1), f0_dst(i, 0))
                        if b == 6:
                            ln_rstd(pool, 1, 0)
            groups(pool, group)

            def low0(first, last):
                for i in range(first, last):
                    low(pool, f0_c, 0, i, f0_dst(i, 1), f0_dst(i, 0))

            ln_rstd(pool, 1, 1)
            low0(F0_K, F0_Q)

            def rms(f):
                pool.wait_ge(ln2_eps, f + 1)
                pool.tensor_tensor(rr[:, 4 * f:4 * f + 4], ve2[:, 4 * f:4 * f + 4], minus_half[:, 0:4], ALU.pow).then_inc(ln2_rr, 1)

            def residual(f):
                for b in range(4 * f, 4 * f + 4):
                    pool.wait_ge(ln_sems[2]["xn"], b + 1)
                    pool.tensor_tensor(x[:, b, :], x[:, b, :], xn[:, b % 2, :], ALU.add).then_inc(ln2_res, 1)

            low0(F0_Q, F0_Y)
            ln_rstd(pool, 2, 0)
            rms(0)
            ln_rstd(pool, 2, 1)
            residual(0)
            rms(1)
            low0(F0_Y, F0_Q1)
            residual(1)
            low0(F0_Q1, F0_N)

            def group1(g, first, last):
                for j in range(GH):
                    for chunks, t, i, what in l1_items(g, j, last):
                        low(pool, chunks, t, i, l1_dst(j, what, 1), l1_dst(j, what, 0))
            groups(pool, group1)
            def low1(t, k, dst):
                pool.wait_ge(f1_high, 3 * t + k + 1)
                pool.tensor_tensor(dst[:, t % 2, 1, :], dq[:, k, :], dst[:, t % 2, 0, :].bitcast(F32), ALU.subtract).then_inc(f1_low, 1)

            low1(0, 0, w_g)
            ln_rstd(pool, 3, 0)
            low1(0, 1, w_u)
            low1(0, 2, w_d)
            ln_rstd(pool, 3, 1)
            for t in range(1, HT):
                for k, w in enumerate((w_g, w_u, w_d)):
                    low1(t, k, w)

        @block.scalar
        def _(act):
            for dst, src in ((m0[:, :], mask0), (qn_w[:, :], q_norm), (kn_w[:, :], k_norm), (m1u[:, :, :], mask1), (shl[:, :], shift_l),
                             (shr[:, :], shift_r), (keys[:, :], f0_keys)):
                act.dma_start(dst, src).then_inc(small_loaded, 16)

            def kv_high(i):
                kv_free(act, i)
                high(act, kv_c, 0, i, kv_dst(i, 0))

            for i in range(12):
                kv_high(i)
            ahead = {1: range(12, 16), 9: range(16, 20), 17: range(20, 24)}
            for i in range(32):
                for c in ahead.get(i, ()):
                    kv_high(c)
                m, b = i // 8, i % 8
                act.wait_ge(kv_mm, i + 1)
                if m < 2:
                    if i >= 4:
                        act.wait_ge(kt_mm, i - 3)
                    act.activation(k_raw[:, i % 4, :], bank[:, i % 2, :], ACT.Copy)
                    if i >= 1:
                        act.wait_ge(k_sum, i)
                    act.activation(k_sq[:, :], bank[:, i % 2, :], ACT.Square).then_inc(kv_out, 1)
                else:
                    act.activation(v0[:, b, (m - 2) * D:(m - 1) * D], bank[:, i % 2, :], ACT.Copy).then_inc(kv_out, 1)
                if 20 <= i < 20 + NB:
                    ln_apply(act, 0, i - 20)
                if 22 <= i < 22 + NB:
                    ln_high(act, 0, i - 22)
            for c in range(4):
                if c == 0:
                    act.wait_ge(kv_mm, 32)
                high(act, q0_c, 0, c, wq_slot(0, 0, c))

            def q_evac(s, b):
                act.wait_ge(q_mm, s + 1)
                if not (isinstance(s, int) and s < 2):
                    act.wait_ge(qt_mm, s - 1)
                act.activation(q_raw[:, b % 2, :], bank[:, 0, :], ACT.Copy).then_inc(q_out, 1)

            q_evac(0, 0)
            q_evac(1, 1)

            def pt_evac(s):
                act.wait_ge(pt_mm, s + 1)
                if not (isinstance(s, int) and s == 0):
                    act.wait_ge(pv_mm, s)
                act.activation(p_t0[:, :], bank[:, 3, :], ACT.Copy).then_inc(pt_out, 1)

            def ot_evac(s, b):
                act.wait_ge(pv_mm, s + 1)
                if not (isinstance(s, int) and s < 2):
                    act.wait_ge(o_mm, s - 1)
                act.activation(o_t0[:, b % 2, 0, :], bank[:, 5, :], ACT.Copy).then_inc(ot_high, 1)

            def high0(i):
                f0_free(act, i)
                high(act, f0_c, 0, i, f0_dst(i, 0))

            def w_highs(g, b, items):
                for chunks, t, i, what, piece in items:
                    l0_free(act, g, b, what, piece)
                    high(act, chunks, t, i, l0_dst(g, what, piece, 0))

            def group(g, first, last):
                for b in range(NB):
                    s = NB * g + b
                    head = first and b == 0
                    if not head:
                        pt_evac(s - 1)
                    items = l0_items(g, b, last)
                    if b == 2:
                        w_highs(g, b, items)
                    act.wait_ge(s_max, s + 1)
                    if not head:
                        act.wait_ge(pt_mm, s)
                    for h in range(GH):
                        e = act.activation(p0[:, h, :], sm0[:, h, :], ACT.Exp, bias=sc0[:, 5, h:h + 1], accum_out=sc0[:, 6, h:h + 1])
                    e.then_inc(p_exp, 1)
                    if not (last and b >= 6):
                        q_evac(s + 2, b)
                    if not head:
                        ot_evac(s - 1, b + 1)
                    if b != 2:
                        w_highs(g, b, items)
                    if last:
                        for i in F0_EARLY.get(b, ()):
                            high0(i)
                        if b == 7:
                            ln_apply(act, 1, 0)
                            ln_apply(act, 1, 1)
            groups(act, group)
            s = NB * GROUPS
            ln_high(act, 1, 0)
            ln_high(act, 1, 1)
            pt_evac(s - 1)
            ln_apply(act, 1, 2)
            ln_apply(act, 1, 3)
            ln_high(act, 1, 2)
            ln_high(act, 1, 3)
            ot_evac(s - 1, 1)
            def r_evac(f):
                act.wait_ge(r_mm, f + 1)
                act.activation(qr[:, f * HALF:(f + 1) * HALF], bank[0:RD, 3, :], ACT.Copy).then_inc(r_out, 1)

            def z_evac(b):
                act.wait_ge(z_mm, b + 1)
                act.activation(z[:, b, :], bank[:, b % 2, :], ACT.Copy).then_inc(z_out, 1)

            ln_apply(act, 1, 4)
            ln_apply(act, 1, 5)
            r_evac(0)
            z_evac(0)
            z_evac(1)
            for b in (4, 5):
                ln_high(act, 1, b)
                ln_apply(act, 1, b + 2)
                z_evac(b - 2)
            ln_high(act, 1, 6)
            ln_high(act, 1, 7)
            r_evac(1)
            for b in range(4, NB):
                high0(F0_K + b - 4)
                z_evac(b)
            act.wait_ge(sub_done, 1)
            act.activation(gate[:, :, :], gate[:, :, :], ACT.Exp).then_inc(exp_done, 1)
            for i in range(F0_K + 4, F0_Q):
                high0(i)
            for b in range(NB):
                act.wait_ge(zt_mm, b + 1)
                if b >= 2:
                    act.wait_ge(f0_mm, b - 1)
                act.activation(z_t[:, b % 2, 0, :], bank[:, 4 + b % 2, :], ACT.Copy).then_inc(zt_high, 1)
                if b == 0:
                    high0(F0_Q)

            def squares(f):
                act.wait_ge(ln_sems[2]["nmr"], f + 1)
                for b in range(4 * f, 4 * f + 4):
                    if b >= 1:
                        act.wait_ge(ln2_ss, b)
                    act.activation(rep1[:, :, :].rearrange("p b e -> p (b e)"), x[:, b, :], ACT.Square, bias=nmr[:, b:b + 1],
                                   scale=rs[:, b:b + 1], accum_out=hs[:, b:b + 1]).then_inc(ln2_ss, 1)

            def apply2(b):
                if b >= 2:
                    act.wait_ge(ln2_res, b - 1)
                    act.wait_ge(ln2_w, b - 1)
                ln_apply(act, 2, b)

            def qk_evac(n, j, k):
                act.wait_ge(q1_mm if k < 2 else k1_mm, 2 * n + k % 2 + 1)
                dst = (q_t1 if k < 2 else k_t1)[:, j % 2, (k % 2) * HALF:(k % 2 + 1) * HALF]
                act.activation(dst, bank[:, k % 2, :], ACT.Copy).then_inc(q1_out if k < 2 else k1_out, 1)

            def v_evac(g, b):
                act.wait_ge(v1_mm, 8 * g + b + 1)
                act.activation(v1[:, b, :], bank[:, 6 + b % 2, :], ACT.Copy).then_inc(v1_out, 1)

            squares(0)
            apply2(0)
            apply2(1)
            qk_evac(0, 0, 2)
            for b in range(4):
                v_evac(0, b)
                ln_high(act, 2, b)
                if b < 2:
                    apply2(b + 2)
            squares(1)
            for i in range(F0_Y, F0_Q1):
                high0(i)
            apply2(4)
            apply2(5)
            qk_evac(0, 0, 3)
            for b in range(4, NB):
                v_evac(0, b)
                ln_high(act, 2, b)
                if b < 6:
                    apply2(b + 2)
            high0(F0_Q1)
            high0(F0_K1)
            qk_evac(0, 0, 0)
            qk_evac(0, 0, 1)

            def group1(g, first, last):
                for j in range(GH):
                    n = 4 * g + j
                    head0 = first and j == 0
                    end = last and j == GH - 1
                    items = l1_items(g, j, last)

                    def item(k):
                        if k < len(items):
                            chunks, t, i, what = items[k]
                            l1_free(act, g, j, what)
                            high(act, chunks, t, i, l1_dst(j, what, 0))

                    for f in range(2):
                        act.wait_ge(s1_floor, 2 * n + f + 1)
                        if not head0:
                            act.wait_ge(pt1_mm, 2 * n - 1 + f)
                        for b in range(4):
                            e = act.activation(p1[:, f, b, :], sm1[:, f, b, :], ACT.Exp, bias=nmx1[:, f, b:b + 1],
                                               accum_out=sum1[:, f, b:b + 1])
                        e.then_inc(p1_exp, 1)
                        if not end:
                            qk_evac(n + 1, j + 1, f)
                        if f == 1:
                            item(0)
                    for f in range(2):
                        act.wait_ge(pt1_mm, 2 * n + f + 1)
                        if not head0:
                            act.wait_ge(pv1_mm, 2 * n - 1 + f)
                        act.activation(p_t1[:, f, :], bank[:, 4, :], ACT.Copy).then_inc(pt1_out, 1)
                        if not end:
                            qk_evac(n + 1, j + 1, 2 + f)
                        act.wait_ge(pv1_mm, 2 * n + f + 1)
                        if not (first and j < 2):
                            act.wait_ge(o1_mm, 16 * g + 8 * (j // 2))
                        act.activation(o_t1[:, j % 2, 0, f * HALF:(f + 1) * HALF], bank[:, 5, :], ACT.Copy).then_inc(ot1_high, 1)
                        if f == 0:
                            item(1)
                    item(2)
                    item(3)
                    if j == GH - 1 and not last:
                        for b in range(NB):
                            v_evac(g + 1, b)
            groups(act, group1)

            def high1(t, k, dst):
                act.wait_ge(scaled, 3 * t + k + 1)
                if t >= 2:
                    if k < 2:
                        act.wait_ge(ab_mm, 4 * (t - 1))
                    else:
                        act.wait_ge(f1_mm, NB * (t - 1))
                act.activation(dst[:, t % 2, 0, :], dq[:, k, :], ACT.Copy).then_inc(f1_high, 1)

            def silu(t, f):
                act.wait_ge(ab_mm, 4 * t + 2 * f + 2)
                if t >= 1:
                    act.wait_ge(h_done, 2 * (t - 1) + f + 1)
                act.activation(sl[:, f, :], bank[:, 2 * f, :], ACT.Silu).then_inc(silu_done, 1)

            def h_split(t, f):
                act.wait_ge(h_done, 2 * t + f + 1)
                if t >= 2:
                    act.wait_ge(f1_mm, NB * (t - 1))
                act.activation(h_t[:, t % 2, 0, f * HALF:(f + 1) * HALF], hf[:, f, :], ACT.Copy).then_inc(h_high, 1)

            high1(0, 0, w_g)
            ln_apply(act, 3, 0)
            ln_apply(act, 3, 1)
            ln_high(act, 3, 0)
            ln_apply(act, 3, 2)
            ln_high(act, 3, 1)
            ln_apply(act, 3, 3)
            act.wait_ge(o1_mm, 4 * H)
            high1(0, 1, w_u)
            high1(0, 2, w_d)
            for b in range(4, NB):
                ln_high(act, 3, b - 2)
                ln_apply(act, 3, b)
            ln_high(act, 3, 6)
            ln_high(act, 3, 7)
            high1(1, 0, w_g)
            high1(1, 1, w_u)
            for t in range(HT):
                for f in range(2):
                    silu(t, f)
                    h_split(t, f)
                if t + 1 < HT:
                    high1(t + 1, 2, w_d)
                if t + 2 < HT:
                    high1(t + 2, 0, w_g)
                    high1(t + 2, 1, w_u)

        @block.vector
        def _(dve):
            def lows(chunks, t, i, dst):
                if chunks.pattern[i] == "D":
                    low(dve, chunks, t, i, dst(1), dst(0))

            for i in range(12):
                lows(kv_c, 0, i, lambda q: kv_dst(i, q))
            dve.wait_ge(small_loaded, 16 * 7)
            dve.scalar_tensor_tensor(qk_w[:, :], qn_w[:, :], float(P) ** 0.5, kn_w[:, :], ALU.mult, ALU.mult).then_inc(qk_w_set, 1)
            dve.wait_ge(qk_w_set, 1)
            for i in range(20):
                if i < 16:
                    dve.wait_ge(kv_out, i + 1)
                    if i >= 1:
                        dve.wait_ge(k_eps, i)
                    dve.tensor_reduce(sc0[:, 0, :], heads4(k_sq[:, :]), AX.X, ALU.add).then_inc(k_sum, 1)
                    dve.wait_ge(k_sum, i + 1)
                    if i >= 1:
                        dve.wait_ge(k_rstd, i)
                    dve.tensor_scalar(sc0[:, 1, :], sc0[:, 0, :], EPS * P, None, ALU.add).then_inc(k_eps, 1)
                if 1 <= i < 17:
                    k = i - 1
                    dve.wait_ge(k_rstd, k + 1)
                    kr = heads4(k_raw[:, k % 4, :])
                    dve.tensor_tensor(kr, kr, over(sc0[:, 2, :], P), ALU.mult).then_inc(k_hat, 1)
                if 3 <= i < 19:
                    k = i - 3
                    m, b = k // 8, k % 8
                    dve.wait_ge(kt_mm, k + 1)
                    dst = k_t[:, :].rearrange("p (g t) -> p g t", g=KVH)[:, 4 * m:4 * m + 4, b * P:(b + 1) * P]
                    dve.tensor_scalar(dst, heads4(bank[:, 2, :]), qk_w[:, 0:1], None, ALU.mult).then_inc(kt_out, 1)

            dve.wait_ge(x_loaded, 16 * NB)
            for b in range(NB):
                ln_stats(dve, 0, b)
            ln_nmr(dve, 0, 0)
            ln_nmr(dve, 0, 1)
            for b in range(NB):
                ln_low(dve, 0, b)
            for c in range(4):
                lows(q0_c, 0, c, lambda q: wq_slot(0, q, c))

            def q_sums(s):
                dve.wait_ge(q_squared, s + 1)
                if not (isinstance(s, int) and s == 0):
                    dve.wait_ge(q_eps, s)
                dve.tensor_reduce(sc0[:, 7, :], heads4(q_sq[:, :]), AX.X, ALU.add).then_inc(q_sum, 1)
                dve.wait_ge(q_sum, s + 1)
                if not (isinstance(s, int) and s == 0):
                    dve.wait_ge(q_rstd, s)
                dve.tensor_scalar(sc0[:, 3, :], sc0[:, 7, :], EPS * P, None, ALU.add).then_inc(q_eps, 1)

            def qt_evac(s):
                dve.wait_ge(qt_mm, s + 1)
                if not (isinstance(s, int) and s == 0):
                    dve.wait_ge(s_mm, s)
                dve.tensor_copy(q_t[:, :], bank[:, 2, :]).then_inc(qt_out, 1)

            q_sums(0)
            q_sums(1)
            qt_evac(0)

            def add_x(s, b):
                dve.wait_ge(o_mm, s + 1)
                dve.tensor_tensor(x[:, b % NB, :], bank[:, 1, :], x[:, b % NB, :], ALU.add).then_inc(x_added, 1)

            def ot_lo(s, b):
                dve.wait_ge(ot_high, s + 1)
                dve.tensor_tensor(o_t0[:, b % 2, 1, :], bank[:, 5, :], o_t0[:, b % 2, 0, :].bitcast(F32), ALU.subtract).then_inc(ot_low, 1)

            def w_lows(g, b, last):
                for chunks, t, i, what, piece in l0_items(g, b, last):
                    if chunks.pattern[i] == "D":
                        low(dve, chunks, t, i, l0_dst(g, what, piece, 1), l0_dst(g, what, piece, 0))

            def group(g, first, last):
                for b in range(NB):
                    s = NB * g + b
                    head = first and b == 0
                    dve.wait_ge(s_mm, s + 1)
                    if not head:
                        dve.wait_ge(p_exp, s)
                    dve.tensor_tensor(sm0[:, :, :], heads4(bank[:, 4, :]), repeat(m0[:, :], GH), ALU.add).then_inc(s_masked, 1)
                    dve.wait_ge(s_masked, s + 1)
                    dve.tensor_reduce(sc0[:, 5, :], sm0[:, :, :], AX.X, ALU.max, negate=True).then_inc(s_max, 1)
                    if not (first and b < 2):
                        dve.wait_ge(pv_mm, s - 1)
                    src = v0[:, b, g * P:(g + 1) * P] if isinstance(g, int) else v0[:, b, bass.ds(g * P, P)]
                    dve.tensor_copy(v_st[:, b % 2, :], src).then_inc(v_staged, 1)
                    if b == 2:
                        w_lows(g, b, last)
                    if not (first and b < 3):
                        if not (first and b == 3):
                            dve.wait_ge(x_added, s - 3)
                        add_x(s - 3, b - 3)
                        if last and b >= 3:
                            dve.wait_ge(x_added, s - 2)
                            ln_stats(dve, 1, b - 3)
                    dve.wait_ge(p_exp, s + 1)
                    if not head:
                        dve.wait_ge(p_norm, s)
                    dve.reciprocal(sc0[:, 0, :], sc0[:, 6, :]).then_inc(p_inv, 1)
                    dve.wait_ge(p_inv, s + 1)
                    dve.tensor_tensor(p0[:, :, :], p0[:, :, :], over(sc0[:, 0, :], P), ALU.mult).then_inc(p_norm, 1)
                    if not (last and b == 7):
                        qt_evac(s + 1)
                    if not head:
                        ot_lo(s - 1, b + 1)
                    if not (last and b >= 6):
                        q_sums(s + 2)
                    if b != 2:
                        w_lows(g, b, last)
                    if last and b == 6:
                        ln_nmr(dve, 1, 0)
            groups(dve, group)
            s = NB * GROUPS
            ln_low(dve, 1, 0)
            ln_low(dve, 1, 1)

            def last_x(b):
                add_x(s - NB + b, b)
                dve.wait_ge(x_added, s - NB + b + 1)
                ln_stats(dve, 1, b)

            last_x(5)
            ln_low(dve, 1, 2)
            ln_low(dve, 1, 3)
            ot_lo(s - 1, 1)
            last_x(6)
            last_x(7)
            ln_nmr(dve, 1, 1)

            for b in range(4, NB):
                ln_low(dve, 1, b)
            dve.wait_ge(sc_mm, 1)
            dve.tensor_copy(scr[:, :, :], bank[:, 2, :].rearrange("p (b e) -> p b e", b=NB)).then_inc(sc_out, 1)
            dve.wait_ge(sc_out, 1)
            for b in range(NB):
                dve.max(top1[:, b, :], scr[:, b, :]).then_inc(t1_done, 1)
            for b in range(NB):
                dve.wait_ge(t1_done, b + 1)
                dve.match_replace(rep1[:, b, :], top1[:, b, :], scr[:, b, :], MASKED).then_inc(rep1_done, 1)
            dve.tensor_tensor(gate[:, :, :], scr[:, :, :], top1[:, :, 0:1].broadcast_to([P, NB, NE]), ALU.subtract).then_inc(sub_done, 1)
            for b in range(NB):
                dve.wait_ge(rep1_done, b + 1)
                dve.max(top2[:, b, :], rep1[:, b, :]).then_inc(t2_done, 1)
            for b in range(NB):
                dve.wait_ge(t2_done, b + 1)
                dve.match_replace(rep2[:, b, :], top2[:, b, :], rep1[:, b, :], MASKED).then_inc(rep2_done, 1)
            dve.wait_ge(rep2_done, NB)
            dve.tensor_tensor(rep2[:, :, :], rep2[:, :, :], scr[:, :, :], ALU.not_equal).then_inc(sel_done, 1)
            dve.wait_ge(sel_done, 1)
            dve.wait_ge(exp_done, 1)
            dve.tensor_tensor(gate[:, :, :], gate[:, :, :], rep2[:, :, :], ALU.mult).then_inc(gated, 1)
            dve.wait_ge(gated, 1)
            dve.tensor_reduce(gsum[:, :], gate[:, :, :], AX.X, ALU.add).then_inc(g_sum, 1)
            dve.wait_ge(g_sum, 1)
            dve.reciprocal(ginv[:, :], gsum[:, :]).then_inc(g_inv, 1)
            dve.wait_ge(g_inv, 1)
            dve.tensor_tensor(gate[:, :, :], gate[:, :, :], over(ginv[:, :], NE), ALU.mult).then_inc(g_done, 1)
            dve.wait_ge(g_done, 1)

            def gate_z(b):
                dve.wait_ge(z_out, b + 1)
                zb = z[:, b, :].rearrange("p (e r) -> p e r", e=NE)
                dve.tensor_tensor(zb, zb, over(gate[:, b, :], RANK), ALU.mult).then_inc(z_gated, 1)

            gate_z(0)
            gate_z(1)
            for b in range(NB):
                if b + 2 < NB:
                    gate_z(b + 2)
                dve.wait_ge(zt_high, b + 1)
                dve.tensor_tensor(z_t[:, b % 2, 1, :], bank[:, 4 + b % 2, :], z_t[:, b % 2, 0, :].bitcast(F32), ALU.subtract).then_inc(zt_low, 1)
                dve.wait_ge(f0_mm, b + 1)
                dve.scalar_tensor_tensor(x[:, b, :], bank[:, 6 + b % 2, :], 2.0, x[:, b, :], ALU.mult, ALU.add).then_inc(f0_added, 1)
                dve.wait_ge(f0_added, b + 1)
                ln_stats(dve, 2, b)
                if b == 5:
                    ln_nmr(dve, 2, 0)

            def rms(f):
                dve.wait_ge(ln2_ss, 4 * f + 4)
                dve.tensor_scalar(ve2[:, 4 * f:4 * f + 4], hs[:, 4 * f:4 * f + 4], 1.0 / D, EPS, ALU.mult, ALU.add).then_inc(ln2_eps, 1)

            def weighted(b):
                dve.wait_ge(ln_sems[2]["xn"], b + 1)
                dve.wait_ge(ln2_rr, b // 4 + 1)
                if b >= 2:
                    dve.wait_ge(ln_sems[2]["tr"], b - 1)
                dve.scalar_tensor_tensor(xw2[:, b % 2, :], xn[:, b % 2, :], rr[:, b:b + 1], lnw[:, :], ALU.mult, ALU.mult).then_inc(ln2_w, 1)

            rms(0)
            dve.wait_ge(lnw_loaded, 16)
            weighted(0)
            weighted(1)
            ln_nmr(dve, 2, 1)
            for b in range(4):
                ln_low(dve, 2, b)
                if b < 2:
                    weighted(b + 2)
            rms(1)
            weighted(4)
            weighted(5)
            for b in range(4, NB):
                ln_low(dve, 2, b)
                if b < 6:
                    weighted(b + 2)

            def unpack(t, k):
                dve.wait_ge(pk_loaded[k], 32 * (t + 1))
                if t >= 1:
                    dve.wait_ge(scaled, 3 * (t - 1) + k + 1)
                if k < 2:
                    dve.tensor_scalar(sh[:, k, :], pk[:, k, :], shl[:, 0:1], shr[:, 0:1], ALU.logical_shift_left,
                                      ALU.arith_shift_right).then_inc(unpacked, 1)
                else:
                    for c in range(4):
                        a = sh[:, k, :].rearrange("p (a c) -> p a c", c=4)[:, :, c]
                        i = pk[:, k, :].rearrange("p (a c) -> p a c", c=4)[:, :, c]
                        u = dve.tensor_scalar(a, i, shl[:, c:c + 1], shr[:, c:c + 1], ALU.logical_shift_left, ALU.arith_shift_right)
                    u.then_inc(unpacked, 1)

            def scale(t, k):
                u = 3 * t + k
                dve.wait_ge(unpacked, u + 1)
                if t >= 1:
                    dve.wait_ge(f1_low, u - 2)
                dve.tensor_tensor(dq[:, k, :], sh[:, k, :], ps[:, k, :], ALU.mult).then_inc(scaled, 1)

            dve.wait_ge(zt_mm, NB)
            dve.tensor_scalar(m1[:, :, :], m1u[:, :, :], -1.0, -MASKED, ALU.add, ALU.mult).then_inc(mask_set, 1)
            dve.wait_ge(mask_set, 1)

            def group1(g, first, last):
                for j in range(GH):
                    n = 4 * g + j
                    head0 = first and j == 0
                    par = j % 2
                    for f in range(2):
                        k = 2 * n + f
                        dve.wait_ge(s1_mm, k + 1)
                        if f == 0:
                            dve.wait_ge(bias_loaded[par], 16 * ((GH // 2) * g + j // 2 + 1))
                        if not head0:
                            dve.wait_ge(p1_exp, k - 1)
                        dve.tensor_tensor(sm1[:, f], bank[:, 2 + f, :].rearrange("p (b n) -> p b n", b=4), repeat(b_sb[:, par, :], 4),
                                          ALU.add).then_inc(s1_biased, 1)
                        dve.wait_ge(s1_biased, k + 1)
                        dve.tensor_tensor(sm1[:, f], sm1[:, f], m1[:, 4 * f:4 * f + 4, :], ALU.add).then_inc(s1_masked, 1)
                        dve.wait_ge(s1_masked, k + 1)
                        dve.tensor_reduce(nmx1[:, f], sm1[:, f], AX.X, ALU.max, negate=True).then_inc(s1_max, 1)
                        dve.wait_ge(s1_max, k + 1)
                        dve.tensor_scalar(nmx1[:, f], nmx1[:, f], -MAX_FLOOR, None, ALU.min).then_inc(s1_floor, 1)
                    for f in range(2):
                        k = 2 * n + f
                        dve.wait_ge(p1_exp, k + 1)
                        dve.tensor_scalar(inv1[:, f], sum1[:, f], 1e-30, None, ALU.max).then_inc(p1_guard, 1)
                        dve.wait_ge(p1_guard, k + 1)
                        dve.reciprocal(inv1[:, f], inv1[:, f]).then_inc(p1_inv, 1)
                        dve.wait_ge(p1_inv, k + 1)
                        dve.tensor_tensor(p1[:, f], p1[:, f], over(inv1[:, f], P), ALU.mult).then_inc(p1_norm, 1)
                    for f in range(2):
                        dve.wait_ge(ot1_high, 2 * n + f + 1)
                        dve.tensor_tensor(o_t1[:, par, 1, f * HALF:(f + 1) * HALF], bank[:, 5, :],
                                          o_t1[:, par, 0, f * HALF:(f + 1) * HALF].bitcast(F32), ALU.subtract).then_inc(ot1_low, 1)
                    if last and j == 3:
                        for k in range(3):
                            unpack(0, k)
                        for k in range(3):
                            scale(0, k)
                    for b in range(NB if j % 2 else 0):
                        u = 16 * g + 8 * (j // 2) + b
                        dve.wait_ge(o1_mm, u + 1)
                        if not (first and j == 1):
                            dve.wait_ge(x1_added, u - 7)
                        elif b == 0:
                            dve.wait_ge(ln2_res, NB)
                        dve.tensor_tensor(x[:, b, :], bank[:, 6 + b % 2, :], x[:, b, :], ALU.add).then_inc(x1_added, 1)
                        if last and j == 3:
                            dve.wait_ge(x1_added, u + 1)
                            ln_stats(dve, 3, b)
                            if b == 5:
                                ln_nmr(dve, 3, 0)
            groups(dve, group1)

            ln_nmr(dve, 3, 1)
            for b in range(2):
                ln_low(dve, 3, b)
            for k in range(3):
                unpack(1, k)
            for b in range(2, NB):
                ln_low(dve, 3, b)
            for k in range(3):
                scale(1, k)
            for t in range(HT + 1):
                if t < HT:
                    for f in range(2):
                        dve.wait_ge(silu_done, 2 * t + f + 1)
                        if t >= 1:
                            dve.wait_ge(h_low, 2 * (t - 1) + f + 1)
                        dve.tensor_tensor(hf[:, f, :], bank[:, 2 * f + 1, :], sl[:, f, :], ALU.mult).then_inc(h_done, 1)
                        dve.wait_ge(h_high, 2 * t + f + 1)
                        dve.tensor_tensor(h_t[:, t % 2, 1, f * HALF:(f + 1) * HALF], hf[:, f, :],
                                          h_t[:, t % 2, 0, f * HALF:(f + 1) * HALF].bitcast(F32), ALU.subtract).then_inc(h_low, 1)
                if t + 2 < HT:
                    for k in range(3):
                        unpack(t + 2, k)
                if t >= 1:
                    for b in range(NB):
                        u = NB * (t - 1) + b
                        dve.wait_ge(f1_mm, u + 1)
                        if t >= 2:
                            dve.wait_ge(f1_added, u - NB + 1)
                        dve.tensor_tensor(x[:, b, :], bank[:, 4 + b % 4, :], x[:, b, :], ALU.add).then_inc(f1_added, 1)
                if t + 2 < HT:
                    for k in range(3):
                        scale(t + 2, k)

        @block.tensor
        def _(pe):
            pe.wait_ge(ident_set, 2)
            for i in range(32):
                m, b = i // 8, i % 8
                before = None
                if i == 0:
                    before = lambda kt: wait_lows(pe, kv_c, 0, 2 * kt, 2 * kt + 1)
                elif i == 4:
                    before = lambda kt: wait_lows(pe, kv_c, 0, 8 + kt, 8 + kt)
                elif b == 0:
                    before = lambda kt: wait_lows(pe, kv_c, 0, 8 + 4 * m + kt, 8 + 4 * m + kt)
                if i >= 2:
                    pe.wait_ge(kv_out, i - 1)
                product(pe, bank[:, i % 2, :], [(l, (kv_slot(m, 0, kt), kv_slot(m, 1, kt))) for kt, l in enumerate(ctx_tile(b))],
                        before=before).then_inc(kv_mm, 1)
                if 3 <= i < 19:
                    k = i - 3
                    pe.wait_ge(k_hat, k + 1)
                    if k >= 1:
                        pe.wait_ge(kt_out, k)
                    transposes(pe, 2, k_raw[:, k % 4, :]).then_inc(kt_mm, 1)
                if 22 <= i < 22 + NB:
                    ln_transpose(pe, 0, i - 22)

            def q_mms(s, b, par, before):
                if not (isinstance(s, int) and s == 0):
                    pe.wait_ge(q_out, s)
                product(pe, bank[:, 0, :], [(l, (wq_slot(par, 0, kt), wq_slot(par, 1, kt))) for kt, l in enumerate(xn_tile(b % NB))],
                        before=before).then_inc(q_mm, 1)

            def q_transposes(s, b):
                pe.wait_ge(q_hat, s + 1)
                if not (isinstance(s, int) and s == 0):
                    pe.wait_ge(qt_out, s)
                transposes(pe, 2, q_raw[:, b % 2, :]).then_inc(qt_mm, 1)

            pe.wait_ge(ln_sems[0]["low"], NB)
            pe.wait_ge(kt_out, 16)
            q_mms(0, 0, 0, lambda kt: wait_lows(pe, q0_c, 0, kt, kt))
            q_mms(1, 1, 0, None)
            q_transposes(0, 0)

            def pt(s):
                pe.wait_ge(p_norm, s + 1)
                if not (isinstance(s, int) and s == 0):
                    pe.wait_ge(pt_out, s)
                transposes(pe, 3, p0[:, :, :].rearrange("p h n -> p (h n)")).then_inc(pt_mm, 1)

            def pv(s, b):
                pe.wait_ge(pt_out, s + 1)
                pe.wait_ge(v_staged, s + 1)
                if not (isinstance(s, int) and s == 0):
                    pe.wait_ge(ot_low, s)
                pe.matmul(bank[:, 5, :], v_st[:, b % 2, :], p_t0[:, :], start=True, stop=True).then_inc(pv_mm, 1)

            def project(s, b, before=None):
                pe.wait_ge(ot_low, s + 1)
                if not (isinstance(s, int) and s == 0):
                    pe.wait_ge(x_added, s)
                product(pe, bank[:, 1, :], [((o_t0[:, b % 2, 0, h * P:(h + 1) * P], o_t0[:, b % 2, 1, h * P:(h + 1) * P]),
                                             (w_o0[:, 0, h, :], w_o0[:, 1, h, :])) for h in range(GH)], before=before).then_inc(o_mm, 1)

            def group(g, first, last):
                for b in range(NB):
                    s = NB * g + b
                    head = first and b == 0
                    pe.wait_ge(qt_out, s + 1)
                    if not head:
                        pe.wait_ge(s_masked, s)
                    at = g * TOK + b * P
                    rhs = k_t[:, at:at + P] if isinstance(at, int) else k_t[:, bass.ds(at, P)]
                    for h in range(GH):
                        mm = pe.matmul(bank[:, 4, h * P:(h + 1) * P], q_t[:, h * P:(h + 1) * P], rhs, start=True, stop=True)
                    mm.then_inc(s_mm, 1)
                    if not head:
                        pt(s - 1)
                    if not (last and b >= 6):
                        if b < 6:
                            q_mms(s + 2, b + 2, g % 2, None)
                        else:
                            need = (lambda kt: wait_lows(pe, l0_c, g, 4 + kt if kt else 0, 4 + kt if kt else 0)) if b == 6 else None
                            q_mms(s + 2, b + 2, (g + 1) % 2, need)
                    if not head:
                        pv(s - 1, b + 1)
                    if not (last and b == 7):
                        q_transposes(s + 1, b + 1)
                    if not (first and b < 2):
                        if b == 2 and last:
                            project(s - 2, b, lambda h: wait_lows(pe, l0e_c, 0, h, h))
                        elif b == 2:
                            project(s - 2, b, lambda h: wait_lows(pe, l0_c, g, 1 + h, 1 + h))
                        else:
                            project(s - 2, b)
            groups(pe, group)
            s = NB * GROUPS
            ln_transpose(pe, 1, 0)
            ln_transpose(pe, 1, 1)
            pt(s - 1)
            ln_transpose(pe, 1, 2)
            ln_transpose(pe, 1, 3)
            pv(s - 1, 1)
            project(s - 2, 0)
            project(s - 1, 1)

            def router(f):
                pe.wait_ge(ln_sems[1]["low"], 4 * f + 4)
                if f == 0:
                    wait_lows(pe, f0_c, 0, F0_R, F0_R)
                else:
                    pe.wait_ge(r_out, 1)
                terms = [((w_r[:, 0, kt * P:(kt + 1) * P], w_r[:, 1, kt * P:(kt + 1) * P]), r) for kt, r in enumerate(xn_half(f))]
                product(pe, bank[:, 3, :], terms).then_inc(r_mm, 1)

            def experts(b):
                if b == 0:
                    wait_lows(pe, f0_c, 0, F0_A, F0_A + 3)
                elif b == 1:
                    pe.wait_ge(x_added, s)
                else:
                    pe.wait_ge(z_out, b - 1)
                product(pe, bank[:, b % 2, :], [(l, (wide[:, 0, kt, 0:D], wide[:, 1, kt, 0:D])) for kt, l in enumerate(xn_tile(b))]).then_inc(z_mm, 1)

            router(0)
            experts(0)
            experts(1)
            ln_transpose(pe, 1, 4)
            ln_transpose(pe, 1, 5)
            experts(2)
            ln_transpose(pe, 1, 6)
            experts(3)
            ln_transpose(pe, 1, 7)
            router(1)
            pe.wait_ge(small_loaded, 16 * 7)
            for b in range(NB):
                pe.wait_ge(r_out, b // 4 + 1)
                mm = pe.matmul(bank[:, 2, b * NE:(b + 1) * NE], qr[:, b * P:(b + 1) * P], keys[:, :], start=True, stop=True)
            mm.then_inc(sc_mm, 1)
            for b in range(4, NB):
                experts(b)

            def zt(b):
                pe.wait_ge(z_gated, b + 1)
                if b >= 2:
                    pe.wait_ge(zt_low, b - 1)
                transposes(pe, 4 + b % 2, z[:, b, :]).then_inc(zt_mm, 1)

            zt(0)
            zt(1)
            wait_lows(pe, f0_c, 0, F0_B, F0_B + 3)
            for b in range(NB):
                pe.wait_ge(zt_low, b + 1)
                if b >= 2:
                    pe.wait_ge(f0_added, b - 1)
                terms = [((z_t[:, b % 2, 0, kt * P:(kt + 1) * P], z_t[:, b % 2, 1, kt * P:(kt + 1) * P]),
                          (wide[:, 0, kt, D:2 * D], wide[:, 1, kt, D:2 * D])) for kt in range(KT)]
                product(pe, bank[:, 6 + b % 2, :], terms).then_inc(f0_mm, 1)
                if b + 2 < NB:
                    zt(b + 2)

            def qk(n, j, k, pieces=range(KT)):
                w = (w_q1 if k < 2 else w_k1)[:, j % 2]
                f = k % 2
                if pieces[0] == 0 and not (isinstance(n, int) and n == 0):
                    if k < 2:
                        pe.wait_ge(k1_out, 2 * n + f - 1)
                    else:
                        pe.wait_ge(q1_out, 2 * n + f + 1)
                tokens = xn_half(f) if k < 2 else [
                    (wide[:, 0, kt, f * HALF:(f + 1) * HALF], wide[:, 1, kt, f * HALF:(f + 1) * HALF]) for kt in range(KT)]
                mm = product(pe, bank[:, f, :], [((w[:, 0, kt * P:(kt + 1) * P], w[:, 1, kt * P:(kt + 1) * P]), tokens[kt]) for kt in pieces],
                             first=pieces[0] == 0, final=pieces[-1] == KT - 1)
                if pieces[-1] == KT - 1:
                    mm.then_inc(q1_mm if k < 2 else k1_mm, 1)

            def values(g, b, first):
                if first:
                    if b >= 2:
                        pe.wait_ge(v1_out, b - 1)
                else:
                    pe.wait_ge(v1_out, 8 * g + b - 1)
                    if b < 2:
                        pe.wait_ge(x1_added, 16 * g - 1 + b)
                product(pe, bank[:, 6 + b % 2, :], [(l, (w_v1[:, 0, kt, :], w_v1[:, 1, kt, :])) for kt, l in enumerate(ctx_tile(b))]
                        ).then_inc(v1_mm, 1)

            wait_lows(pe, f0_c, 0, F0_K, F0_Q - 1)
            pe.wait_ge(z_out, NB)
            qk(0, 0, 2)
            pe.wait_ge(f0_added, NB)
            for f in range(2):
                if f == 1:
                    wait_lows(pe, f0_c, 0, F0_Y, F0_Q1 - 1)
                    qk(0, 0, 3)
                for b in range(4 * f, 4 * f + 4):
                    values(0, b, True)
                    ln_transpose(pe, 2, b, xw2, ln2_w)
            pe.wait_ge(ln_sems[2]["low"], 4)
            pe.wait_ge(k1_out, 1)
            qk(0, 0, 0)
            pe.wait_ge(ln_sems[2]["low"], NB)
            pe.wait_ge(k1_out, 2)
            qk(0, 0, 1)

            def group1(g, first, last):
                for j in range(GH):
                    n = 4 * g + j
                    head0 = first and j == 0
                    end = last and j == GH - 1
                    for f in range(2):
                        pe.wait_ge(q1_out, 2 * n + f + 1)
                        pe.wait_ge(k1_out, 2 * n + f + 1)
                        if not head0:
                            pe.wait_ge(s1_biased, 2 * n - 1 + f)
                        elif f == 0:
                            pe.wait_ge(ln_sems[2]["low"], NB)
                        for b in range(4):
                            at = (4 * f + b) * P
                            mm = pe.matmul(bank[:, 2 + f, b * P:(b + 1) * P], q_t1[:, j % 2, at:at + P], k_t1[:, j % 2, at:at + P],
                                           start=True, stop=True)
                        mm.then_inc(s1_mm, 1)
                    if not end:
                        if first and j == 0:
                            wait_lows(pe, f0_c, 0, F0_Q1, F0_K1)
                        elif last and j >= 1:
                            wait_lows(pe, l1e_c, 0, L1E[(j - 1, "q")], L1E[(j - 1, "k")])
                        elif j == 0:
                            wait_lows(pe, l1_c, g - 1, 13, 14)
                        else:
                            wait_lows(pe, l1_c, g, 4 * j - 3, 4 * j - 2)
                        qk(n + 1, j + 1, 0)
                        qk(n + 1, j + 1, 1)
                        qk(n + 1, j + 1, 2, range(0, 2))
                    for f in range(2):
                        pe.wait_ge(p1_norm, 2 * n + f + 1)
                        if not (head0 and f == 0):
                            pe.wait_ge(pt1_out, 2 * n + f)
                        transposes(pe, 4, p1[:, f].rearrange("p b n -> p (b n)")).then_inc(pt1_mm, 1)
                        if not end:
                            if f == 0:
                                qk(n + 1, j + 1, 2, range(2, 4))
                            else:
                                qk(n + 1, j + 1, 3)
                        pe.wait_ge(pt1_out, 2 * n + f + 1)
                        if not (head0 and f == 0):
                            pe.wait_ge(ot1_low, 2 * n + f)
                        if j == 0 and f == 0:
                            pe.wait_ge(v1_out, 8 * g + 8)
                        for b in range(4):
                            mm = pe.matmul(bank[:, 5, b * P:(b + 1) * P], v1[:, 4 * f + b, j * P:(j + 1) * P], p_t1[:, f, b * P:(b + 1) * P],
                                           start=True, stop=True)
                        mm.then_inc(pv1_mm, 1)
                    if j % 2:
                        if last:
                            wait_lows(pe, l1e_c, 0, L1E[(j, "o")], L1E[(j, "o")])
                        else:
                            wait_lows(pe, l1_c, g, 4 * j, 4 * j)
                    for b in range(NB if j % 2 else 0):
                        pe.wait_ge(ot1_low, 2 * n + b // 4 + 1)
                        u = 16 * g + 8 * (j // 2) + b
                        if not (first and j == 1 and b < 2):
                            pe.wait_ge(x1_added, u - 1)
                        if j == 1 and b < 2:
                            pe.wait_ge(v1_out, 8 * g + 8)
                        terms = [((o_t1[:, h, 0, b * P:(b + 1) * P], o_t1[:, h, 1, b * P:(b + 1) * P]), (w_o1[:, h, 0, :], w_o1[:, h, 1, :]))
                                 for h in range(2)]
                        product(pe, bank[:, 6 + b % 2, :], terms).then_inc(o1_mm, 1)
                    if j == GH - 1 and not last:
                        wait_lows(pe, l1_c, g, 15, 15)
                        for b in range(NB):
                            values(g + 1, b, False)
            groups(pe, group1)

            for b in range(4):
                ln_transpose(pe, 3, b)

            def gate_up(t):
                pe.wait_ge(f1_low, 3 * t + 2)
                for f in range(2):
                    if t == 0 and f == 0:
                        pe.wait_ge(ln_sems[3]["low"], 4)
                    if t == 0 and f == 1:
                        for b in range(4, NB):
                            ln_transpose(pe, 3, b)
                        pe.wait_ge(ln_sems[3]["low"], NB)
                    for k, w in enumerate((w_g, w_u)):
                        if t >= 1:
                            pe.wait_ge(h_done, 2 * (t - 1) + f + 1)
                        terms = [((w[:, t % 2, 0, kt * P:(kt + 1) * P], w[:, t % 2, 1, kt * P:(kt + 1) * P]), r) for kt, r in enumerate(xn_half(f))]
                        product(pe, bank[:, 2 * f + k, :], terms).then_inc(ab_mm, 1)

            gate_up(0)
            for t in range(HT):
                if t + 1 < HT:
                    gate_up(t + 1)
                pe.wait_ge(f1_low, 3 * t + 3)
                for b in range(NB):
                    u = NB * t + b
                    pe.wait_ge(h_low, 2 * t + b // 4 + 1)
                    if u >= 4:
                        pe.wait_ge(f1_added, u - 3)
                    product(pe, bank[:, 4 + b % 4, :], [((h_t[:, t % 2, 0, b * P:(b + 1) * P], h_t[:, t % 2, 1, b * P:(b + 1) * P]),
                                                         (w_d[:, t % 2, 0, :], w_d[:, t % 2, 1, :]))]).then_inc(f1_mm, 1)


def kernel(**inputs):
    import numpy as np
    import concourse.bacc as bacc
    from concourse.bass_utils import run_bass_kernel_spmd

    a = {k: np.asarray(v) for k, v in inputs.items()}

    def columns(w):
        return w.reshape(-1, D, KT, P).transpose(0, 2, 3, 1)

    def heads(w):
        return w.reshape(-1, P, KT, P).transpose(0, 3, 2, 1).reshape(-1, P, D)

    def outs(w):
        return w.reshape(D, -1, P).transpose(1, 2, 0)

    def filled(w, rows):
        full = np.zeros((rows,) + w.shape[1:], w.dtype)
        full[: w.shape[0]] = w
        return full

    def both(w):
        return np.stack([w, w], axis=1).reshape(-1)

    hidden = HT * P
    gate_up = {}
    for n in ("1", "3"):
        gate_up["p" + n] = heads(filled(both(a["L1_ffn_w" + n]).reshape(HID, D), hidden))
        gate_up["s" + n] = heads(filled(np.repeat(a["L1_ffn_s" + n], 64).reshape(HID, D), hidden))
    down_p = filled(both(a["L1_ffn_w2"]).reshape(D, HID).T, hidden).reshape(HT, P, D)
    down_s = filled(np.repeat(a["L1_ffn_s2"], 64).reshape(D, HID).T, hidden).reshape(HT, P, D)
    lower = (np.arange(P)[:, None] + HID * np.arange(4)[None, :]) % P >= 64
    arrays = {
        "x_in": a["x"],
        "mask0": a["mask_1x1xSxS2_ff0"].reshape(P, P),
        "mask1": a["mask_BxSxS2_bk0"].transpose(1, 0, 2),
        "ctx_t": a["ctx_4096"].reshape(2, HALF, KT, P).transpose(0, 2, 3, 1),
        "l0_q": columns(a["L0_xattn_Wq"]), "l0_k": columns(a["L0_xattn_Wk"]), "l0_v": columns(a["L0_xattn_Wv"]),
        "l0_o": outs(a["L0_xattn_Wo"]),
        "q_norm": a["L0_xattn_q_norm_w"].reshape(P, 1), "k_norm": a["L0_xattn_k_norm_w"].reshape(P, 1),
        "f0_a": columns(a["L0_ffn_A_w"]), "f0_b": columns(a["L0_ffn_B_w"]),
        "f0_r": heads(filled(a["L0_ffn_Wq_w"], P))[0], "f0_keys": a["L0_ffn_keys"].T,
        "bias": a["L1_xattn_position_bias"], "ln_w": a["L1_xattn_ln_weight"].reshape(1, D),
        "l1_q": heads(a["L1_xattn_w_q"]), "l1_k": heads(a["L1_xattn_w_k"]), "l1_v": columns(a["L1_xattn_w_v"]),
        "l1_o": outs(a["L1_xattn_w_out"]),
        "f1_p1": gate_up["p1"], "f1_s1": gate_up["s1"], "f1_p3": gate_up["p3"], "f1_s3": gate_up["s3"],
        "f1_p2": down_p, "f1_s2": down_s,
        "shift_l": np.where(lower, 28, 0).astype(np.int32), "shift_r": np.where(lower, 28, 4).astype(np.int32),
    }
    nc = bacc.Bacc("TRN2", target_bir_lowering=False, num_devices=1)
    feed, args = {}, {}
    for name, v in arrays.items():
        feed[name + "_dram"] = np.ascontiguousarray(v)
        args[name] = nc.dram_tensor(name + "_dram", v.shape, mybir.dt.from_np(v.dtype), kind="ExternalInput").ap()
    args["out"] = nc.dram_tensor("out_dram", (NB, P, D), F32, kind="ExternalOutput").ap()
    two_layer_block(nc, **args)
    r = run_bass_kernel_spmd(nc, [feed], core_ids=[0])
    return r.results[0]["out_dram"]
```

```python
from contextlib import ExitStack

import concourse.bass as bass
from concourse import mybir

F32 = mybir.dt.float32
F32R = mybir.dt.float32r
I32 = mybir.dt.int32
U8 = mybir.dt.uint8
ALU = mybir.AluOpType
ACT = mybir.ActivationFunctionType
AX = mybir.AxisListType

P = 128
D = 512
KT = D // P
NB = 8
TOK = NB * P
HALF = TOK // 2
H = 32
KVH = 8
GH = H // KVH
GROUPS = H // GH
NE, RANK, RD = 64, 8, 16
HID = 1376
HT = -(-HID // P)
EPS = 1e-5
MASKED = -3.0e38
MAX_FLOOR = -1.0e37
RAW = 4


class Chunks:

    def __init__(self, before, pattern, times=1):
        self.pattern, self.times = pattern, times
        self.c0, self.p0, self.d0 = (before.c1, before.p1, before.d1) if before else (0, 0, 0)
        self.n, self.np, self.nd = len(pattern), pattern.count("P"), pattern.count("D")
        self.c1 = self.c0 + self.n * times
        self.p1 = self.p0 + self.np * times
        self.d1 = self.d0 + self.nd * times

    def slot(self, i):
        return (self.c0 + i) % RAW

    def loaded(self, t, i):
        return (t * (self.n // RAW) + (self.c0 + i) // RAW + 1) * 16

    def high(self, t, i):
        return t * self.n + (self.c0 + i + 1)

    def low(self, t, i):
        kind = self.pattern[i]
        done = self.pattern[: i + 1].count(kind)
        if kind == "P":
            return "P", t * self.np + (self.p0 + done)
        return "D", t * self.nd + (self.d0 + done)


def two_layer_block(
    nc, x_in, mask0, mask1, ctx_t, l0_q, l0_k, l0_v, l0_o, q_norm, k_norm, f0_a, f0_b, f0_r, f0_keys,
    bias, ln_w, l1_q, l1_k, l1_v, l1_o, f1_p1, f1_s1, f1_p3, f1_s3, f1_p2, f1_s2, shift_l, shift_r, out,
):
    kv_c = Chunks(None, "PDPD" "DD" + "P" * 14)
    q0_c = Chunks(kv_c, "PDPD")
    l0_c = Chunks(q0_c, "PPDDDPPP", GROUPS - 1)
    l0e_c = Chunks(l0_c, "PDDD")
    F0_R, F0_A, F0_Y, F0_B, F0_K, F0_V, F0_X, F0_Q, F0_Q1, F0_K1, F0_N = 0, 1, 5, 9, 13, 14, 18, 22, 23, 24, 25
    f0_c = Chunks(l0e_c, "P" * F0_N)
    l1_c = Chunks(f0_c, "PPPP" * GH, GROUPS - 1)
    l1e_c = Chunks(l1_c, "PPP" "PPP" "P" "P")
    L1E = {(0, "o"): 0, (0, "q"): 1, (0, "k"): 2, (1, "o"): 3, (1, "q"): 4, (1, "k"): 5, (2, "o"): 6, (3, "o"): 7}

    with ExitStack() as top:
        def alloc(stack, name, shape, dt=F32):
            return stack.enter_context(nc.sbuf_tensor(name, shape, dt))

        def sem(name):
            return top.enter_context(nc.semaphore(name))

        x = alloc(top, "x", [P, NB, D])
        xn_t = alloc(top, "xn_t", [P, 2, KT, TOK], F32R)
        wide = alloc(top, "wide", [P, 2, KT, TOK], F32R)
        raw = alloc(top, "raw", [P, RAW, D])
        ident = alloc(top, "ident", [P, P])
        m0 = alloc(top, "m0", [P, P])
        m1u = alloc(top, "m1u", [P, NB, P], U8)
        w_r = alloc(top, "w_r", [P, 2, D], F32R)
        keys = alloc(top, "keys", [RD, NE])
        qn_w = alloc(top, "qn_w", [P, 1])
        kn_w = alloc(top, "kn_w", [P, 1])
        qk_w = alloc(top, "qk_w", [P, 1])
        minus_half = alloc(top, "minus_half", [P, NB])
        st = alloc(top, "st", [P, NB, 6])
        mv = alloc(top, "mv", [P, NB, 2])
        xn = alloc(top, "xn", [P, 2, D])
        ve = alloc(top, "ve", [P, NB])
        ve2 = alloc(top, "ve2", [P, NB])
        rs = alloc(top, "rs", [P, NB])
        nmr = alloc(top, "nmr", [P, NB])
        hs = alloc(top, "hs", [P, NB])
        rr = alloc(top, "rr", [P, NB])
        shl = alloc(top, "shl", [P, 4], I32)
        shr = alloc(top, "shr", [P, 4], I32)
        sc0 = alloc(top, "sc0", [P, 8, GH])

        with ExitStack() as s:
            v0 = alloc(s, "v0", [P, NB, KVH * P])
            k_t = alloc(s, "k_t", [P, KVH * TOK])
            w_o0 = alloc(s, "w_o0", [P, 2, GH, D], F32R)
            with ExitStack() as s2:
                kv_w1 = alloc(s2, "kv_w1", [P, 2, KT, D], F32R)
                k_raw = alloc(s2, "k_raw", [P, 4, D])
                k_sq = alloc(s2, "k_sq", [P, D])
            with ExitStack() as s2:
                sm0 = alloc(s2, "sm0", [P, GH, P])
                p0 = alloc(s2, "p0", [P, GH, P])
                p_t0 = alloc(s2, "p_t0", [P, 2, D], F32R)
                o_t0 = alloc(s2, "o_t0", [P, 2, 2, D], F32R)
                q_raw = alloc(s2, "q_raw", [P, 2, D])
                q_sq = alloc(s2, "q_sq", [P, D])
                q_t = alloc(s2, "q_t", [P, D])
                v_st = alloc(s2, "v_st", [P, 2, 2, P], F32R)
        with ExitStack() as s:
            w_q1 = alloc(s, "w_q1", [P, 2, 2, D], F32R)
            w_k1 = alloc(s, "w_k1", [P, 2, 2, D], F32R)
            w_v1 = alloc(s, "w_v1", [P, 2, KT, D], F32R)
            w_o1 = alloc(s, "w_o1", [P, 2, 2, D], F32R)
            k_t1 = alloc(s, "k_t1", [P, 2, TOK])
            v1 = alloc(s, "v1", [P, NB, D])
            with ExitStack() as s2:
                z = alloc(s2, "z", [P, NB, D])
                z_t = alloc(s2, "z_t", [P, 2, 2, D], F32R)
                qr = alloc(s2, "qr", [RD, TOK])
                scr = alloc(s2, "scr", [P, NB, NE])
                top1 = alloc(s2, "top1", [P, NB, 8])
                top2 = alloc(s2, "top2", [P, NB, 8])
                rep1 = alloc(s2, "rep1", [P, NB, NE])
                rep2 = alloc(s2, "rep2", [P, NB, NE])
                gate = alloc(s2, "gate", [P, NB, NE])
                gsum = alloc(s2, "gsum", [P, NB])
                ginv = alloc(s2, "ginv", [P, NB])
                xw2 = alloc(s2, "xw2", [P, 2, D])
                lnw = alloc(s2, "lnw", [P, D])
            with ExitStack() as s2:
                m1 = alloc(s2, "m1", [P, NB, P])
                q_t1 = alloc(s2, "q_t1", [P, 2, TOK])
                sm1 = alloc(s2, "sm1", [P, 2, 4, P])
                p1 = alloc(s2, "p1", [P, 2, 4, P])
                p_t1 = alloc(s2, "p_t1", [P, 2, D])
                o_t1 = alloc(s2, "o_t1", [P, 2, 2, TOK], F32R)
                b_sb = alloc(s2, "b_sb", [P, 2, P])
                nmx1 = alloc(s2, "nmx1", [P, 2, 4])
                sum1 = alloc(s2, "sum1", [P, 2, 4])
                inv1 = alloc(s2, "inv1", [P, 2, 4])
        with ExitStack() as s:
            pk = alloc(s, "pk", [P, 3, D], I32)
            ps = alloc(s, "ps", [P, 3, D])
            sh = alloc(s, "sh", [P, 3, D], I32)
            dq = alloc(s, "dq", [P, 3, D])
            w_g = alloc(s, "w_g", [P, 2, 2, D], F32R)
            w_d = alloc(s, "w_d", [P, 2, 2, D], F32R)
            w_u = alloc(s, "w_u", [P, 2, 2, D], F32R)
            h_t = alloc(s, "h_t", [P, 2, 2, TOK], F32R)
            sl = alloc(s, "sl", [P, 2, HALF])
            hf = alloc(s, "hf", [P, 2, HALF])
        bank = top.enter_context(nc.psum_tensor("bank", [P, 8, 512], F32))

        ctx_loaded, ctx_high, ctx_low = [sem(f"ctx_loaded{i}") for i in range(4)], sem("ctx_high"), sem("ctx_low")
        raw_loaded = [sem(f"raw_loaded{i}") for i in range(RAW)]
        w_high, w_low_p, w_low_d = sem("w_high"), sem("w_low_pool"), sem("w_low_vector")
        x_loaded, small_loaded, lnw_loaded = sem("x_loaded"), sem("small_loaded"), sem("lnw_loaded")
        ones_set, ident_set, qk_w_set, mask_set = sem("ones_set"), sem("ident_set"), sem("qk_w_set"), sem("mask_set")
        kv_mm, kv_out, k_sum, k_eps, k_rstd, k_hat, kt_mm, kt_out = (
            sem(n) for n in ("kv_mm", "kv_out", "k_sum", "k_eps", "k_rstd", "k_hat", "kt_mm", "kt_out"))
        ln_sems = [{n: sem(f"ln{i}_{n}") for n in ("stats", "aggr", "eps", "rstd", "nmr", "xn", "tr", "high", "low")} for i in range(4)]
        ln2_ss, ln2_eps, ln2_rr, ln2_res, ln2_w = (sem("ln2_" + n) for n in ("ss", "e2", "rr", "res", "w"))
        (q_mm, q_out, q_squared, q_sum, q_eps, q_rstd, q_hat, qt_mm, qt_out, s_mm, s_masked, s_max, p_exp, p_inv, p_norm,
         pt_mm, pt_out, pt_low, v_high, v_staged, pv_mm, ot_high, ot_low, o_mm, x_added) = (
            sem("a0_" + n) for n in (
                "q_mm", "q_out", "q_squared", "q_sum", "q_eps", "q_rstd", "q_hat", "qt_mm", "qt_out", "s_mm", "s_masked",
                "s_max", "p_exp", "p_inv", "p_norm", "pt_mm", "pt_out", "pt_low", "v_high", "v_staged", "pv_mm", "ot_high", "ot_low", "o_mm", "x_added"))
        (r_mm, r_out, sc_mm, sc_out, t1_done, rep1_done, t2_done, rep2_done, sel_done, sub_done, exp_done, gated, g_sum, g_inv,
         g_done, z_mm, z_out, z_gated, zt_mm, zt_high, zt_low, f0_mm, f0_added) = (
            sem("f0_" + n) for n in (
                "r_mm", "r_out", "sc_mm", "sc_out", "t1", "rep1", "t2", "rep2", "sel", "sub", "exp", "gated", "sum", "inv",
                "gate", "z_mm", "z_out", "z_gated", "zt_mm", "zt_high", "zt_low", "mm", "added"))
        (q1_mm, k1_mm, q1_out, k1_out, v1_mm, v1_out, s1_mm, s1_biased, s1_masked, s1_max, s1_floor, p1_exp, p1_guard, p1_inv, p1_norm, pt1_mm, pt1_out,
         pv1_mm, ot1_high, ot1_low, o1_mm, x1_added) = (
            sem("a1_" + n) for n in (
                "q_mm", "k_mm", "q_out", "k_out", "v_mm", "v_out", "s_mm", "s_biased", "s_masked", "s_max", "s_floor", "p_exp", "p_guard", "p_inv", "p_norm",
                "pt_mm", "pt_out", "pv_mm", "ot_high", "ot_low", "o_mm", "x_added"))
        bias_loaded = [sem(f"bias_loaded{i}") for i in range(2)]
        pk_loaded = [sem(f"packed_loaded{i}") for i in range(3)]
        unpacked, scaled, f1_high, f1_low, ab_mm, silu_done, h_done, h_high, h_low, f1_mm, f1_added = (
            sem("f1_" + n) for n in ("unpacked", "scaled", "high", "low", "ab_mm", "silu", "h", "h_high", "h_low", "mm", "added"))
        stored = sem("stored")

        block = top.enter_context(nc.Block())

        def wait_low(eng, chunks, t, i):
            kind, n = chunks.low(t, i)
            eng.wait_ge(w_low_p if kind == "P" else w_low_d, n)

        def wait_lows(eng, chunks, t, first, last):
            for kind in "PD":
                own = [i for i in range(first, last + 1) if chunks.pattern[i] == kind]
                if own:
                    wait_low(eng, chunks, t, own[-1])

        def load(sp, chunks, t, i, src):
            r = i - RAW
            if isinstance(t, int) and chunks.c0 + t * chunks.n + r < 0:
                pass
            elif r >= 0:
                wait_low(sp, chunks, t, r)
            else:
                before, tb, ib = owner(chunks, t, r)
                wait_low(sp, before, tb, ib)
            sp.dma_start(raw[:, chunks.slot(i), :], src).then_inc(raw_loaded[chunks.slot(i)], 16)

        order = [kv_c, q0_c, l0_c, l0e_c, f0_c, l1_c, l1e_c]

        def owner(chunks, t, r):
            if not isinstance(t, int) or t > 0:
                assert -r <= chunks.n
                return chunks, t - 1, chunks.n + r
            k = order.index(chunks) - 1
            while -r > order[k].n * order[k].times:
                r += order[k].n * order[k].times
                k -= 1
            b = order[k]
            at = b.n * b.times + r
            return b, at // b.n, at % b.n

        def high(act, chunks, t, i, dst):
            act.wait_ge(raw_loaded[chunks.slot(i)], chunks.loaded(t, i))
            act.activation(dst, raw[:, chunks.slot(i), :], ACT.Copy).then_inc(w_high, 1)

        def low(eng, chunks, t, i, dst, dst_high):
            eng.wait_ge(w_high, chunks.high(t, i))
            eng.tensor_tensor(dst, raw[:, chunks.slot(i), :], dst_high.bitcast(F32), ALU.subtract).then_inc(
                w_low_p if chunks.pattern[i] == "P" else w_low_d, 1)

        def product(pe, dst, terms, first=True, final=True, before=None):
            n = len(terms)
            for k, ((lh, ll), (rh, rl)) in enumerate(terms):
                if before:
                    before(k)
                pe.matmul(dst, lh, rh, start=(first and k == 0), stop=False)
                pe.matmul(dst, lh, rl, start=False, stop=False)
                last = pe.matmul(dst, ll, rh, start=False, stop=(final and k == n - 1))
            return last

        def xn_tile(b):
            return [(xn_t[:, 0, kt, b * P:(b + 1) * P], xn_t[:, 1, kt, b * P:(b + 1) * P]) for kt in range(KT)]

        def xn_half(f):
            return [(xn_t[:, 0, kt, f * HALF:(f + 1) * HALF], xn_t[:, 1, kt, f * HALF:(f + 1) * HALF]) for kt in range(KT)]

        def ctx_tile(b):
            return [(wide[:, 0, kt, b * P:(b + 1) * P], wide[:, 1, kt, b * P:(b + 1) * P]) for kt in range(KT)]

        def heads4(ap):
            return ap.rearrange("p (h n) -> p h n", h=GH)

        def over(ap, n):
            return ap.unsqueeze(2).broadcast_to([P, ap.shape[1], n])

        def repeat(ap, n):
            return ap.unsqueeze(1).broadcast_to([P, n, ap.shape[1]])

        def transposes(pe, dst, src):
            for k in range(4):
                last = pe.transpose(bank[:, dst, k * P:(k + 1) * P], src[:, k * P:(k + 1) * P], ident[:, :])
            return last

        LN_BANKS = ((4, 5), (6, 7), (2, 3), (4, 5))

        LAST_BANKS = (6, 7, 0, 1, 2, 3, 6, 7)

        def ln_stats(dve, i, b):
            L = ln_sems[i]
            dve.bn_stats(st[:, b, :], x[:, b, :]).then_inc(L["stats"], 1)
            dve.wait_ge(L["stats"], b + 1)
            dve.bn_aggr(mv[:, b, :], st[:, b, :]).then_inc(L["aggr"], 1)
            if b % 4 == 3:
                dve.wait_ge(L["aggr"], b + 1)
                dve.tensor_scalar(ve[:, b - 3:b + 1], mv[:, b - 3:b + 1, 1], EPS, None, ALU.add).then_inc(L["eps"], 1)

        def ln_rstd(pool, i, f):
            L = ln_sems[i]
            pool.wait_ge(L["eps"], f + 1)
            pool.tensor_tensor(rs[:, 4 * f:4 * f + 4], ve[:, 4 * f:4 * f + 4], minus_half[:, 0:4], ALU.pow).then_inc(L["rstd"], 1)

        def ln_nmr(dve, i, f):
            L = ln_sems[i]
            dve.wait_ge(L["rstd"], f + 1)
            dve.scalar_tensor_tensor(nmr[:, 4 * f:4 * f + 4], mv[:, 4 * f:4 * f + 4, 0], -1.0, rs[:, 4 * f:4 * f + 4],
                                     ALU.mult, ALU.mult).then_inc(L["nmr"], 1)

        def ln_apply(act, i, b):
            L = ln_sems[i]
            act.wait_ge(L["nmr"], b // 4 + 1)
            if b >= 2:
                act.wait_ge(L["tr"], b - 1)
            act.activation(xn[:, b % 2, :], x[:, b, :], ACT.Identity, bias=nmr[:, b:b + 1], scale=rs[:, b:b + 1]).then_inc(L["xn"], 1)

        def ln_transpose(pe, i, b, src=None, ready=None):
            L = ln_sems[i]
            pe.wait_ge(ready or L["xn"], b + 1)
            if b >= 2:
                pe.wait_ge(L["low"], b - 1)
            transposes(pe, LN_BANKS[i][b % 2], (src or xn)[:, b % 2, :]).then_inc(L["tr"], 1)

        def ln_high(act, i, b):
            L = ln_sems[i]
            act.wait_ge(L["tr"], b + 1)
            act.activation(xn_t[:, 0, :, b * P:(b + 1) * P], heads4(bank[:, LN_BANKS[i][b % 2], :]), ACT.Copy).then_inc(L["high"], 1)

        def ln_low(dve, i, b):
            L = ln_sems[i]
            dve.wait_ge(L["high"], b + 1)
            dve.tensor_tensor(xn_t[:, 1, :, b * P:(b + 1) * P], heads4(bank[:, LN_BANKS[i][b % 2], :]),
                              xn_t[:, 0, :, b * P:(b + 1) * P].bitcast(F32), ALU.subtract).then_inc(L["low"], 1)

        def kv_slot(m, part, kt):
            return (w_o0 if m % 2 == 0 else kv_w1)[:, part, kt, :]

        def kv_what(i):
            if i < 4:
                return "w", 0, i
            return ("ctx", 1, i - 4) if i < 8 else ("w", 1 + (i - 8) // 4, i % 4)

        def kv_dst(i, part):
            what, m, kt = kv_what(i)
            return wide[:, part, kt, m * HALF:(m + 1) * HALF] if what == "ctx" else kv_slot(m, part, kt)

        def kv_src(i):
            what, m, kt = kv_what(i)
            return ctx_t[m, kt] if what == "ctx" else (l0_k if m < 2 else l0_v)[m % 2, kt]

        KV_AHEAD = {i: c for first, chunk, n in ((0, 6, 6), (9, 12, 4), (17, 16, 4)) for i, c in zip(range(first, first + n), range(chunk, chunk + n))}

        def kv_bank(i):
            return i % 2 if i < 28 else 6 + i % 2

        def kv_free(eng, i):
            if i == 12:
                eng.wait_ge(kv_mm, 8)
            if i == 16:
                eng.wait_ge(kv_mm, 16)

        def wq_slot(par, part, kt):
            if isinstance(par, int):
                return wide[:, part, kt, par * D:(par + 1) * D]
            return wide[:, part, kt, bass.ds(par * D, D)]

        L0_ITEMS = [("q", 0, 0), ("o", 0, 1), ("o", 1, 1), ("o", 2, 2), ("o", 3, 2), ("q", 1, 3), ("q", 2, 4), ("q", 3, 5)]

        def l0_items(g, b, last):
            if last:
                return [(l0e_c, 0, k, "o", k) for k, bb in enumerate((1, 1, 2, 2)) if bb == b]
            return [(l0_c, g, k, what, piece) for k, (what, piece, bb) in enumerate(L0_ITEMS) if bb == b]

        def l0_dst(g, what, piece, part):
            return w_o0[:, part, piece, :] if what == "o" else wq_slot((g + 1) % 2, part, piece)

        def l0_free(eng, g, b, what, piece):
            first = isinstance(g, int) and g == 0
            if what == "q" and piece == 0 and first:
                eng.wait_ge(kv_mm, 32)
            if what == "o" and piece == 0:
                if first:
                    eng.wait_ge(kv_mm, 32)
                else:
                    eng.wait_ge(o_mm, 8 * g)

        def f0_dst(i, part):
            if i == F0_R:
                return w_r[:, part, :]
            if i < F0_Y:
                return wide[:, part, i - F0_A, 0:D]
            if i < F0_B:
                return wide[:, part, i - F0_Y, HALF:TOK]
            if i < F0_K:
                return expert_out(i - F0_B, part)
            if F0_V <= i < F0_X:
                return w_v1[:, part, i - F0_V, :]
            if F0_X <= i < F0_Q:
                return wide[:, part, i - F0_X, 0:HALF]
            w, head = {F0_K: (w_k1, 0), F0_Q: (w_q1, 0), F0_Q1: (w_q1, 1), F0_K1: (w_k1, 1)}[i]
            return w[:, head, part, :]

        def expert_out(piece, part):
            return (w_o1 if piece < 2 else w_q1)[:, piece % 2, part, :]

        def f0_src(i):
            if i == F0_R:
                return f0_r
            if i < F0_Y:
                return f0_a[0, i - F0_A]
            if i < F0_B:
                return ctx_t[1, i - F0_Y]
            if i < F0_K:
                return f0_b[0, i - F0_B]
            if F0_V <= i < F0_X:
                return l1_v[0, i - F0_V]
            if F0_X <= i < F0_Q:
                return ctx_t[0, i - F0_X]
            return {F0_K: l1_k[0], F0_Q: l1_q[0], F0_Q1: l1_q[1], F0_K1: l1_k[1]}[i]

        def f0_free(eng, i):
            if i == F0_A:
                eng.wait_ge(q_mm, 56)
            if i == F0_Y:
                eng.wait_ge(q_mm, 64)
            if i == F0_B:
                eng.wait_ge(o_mm, 64)
            if i == F0_X:
                eng.wait_ge(z_mm, NB)
            if i == F0_Q:
                eng.wait_ge(f0_mm, NB)

        V_ORDER = (4, 5, 6, 7, 0, 1, 2, 3)

        def v0_bank(k):
            return 0 if k == 0 else 7 - k % 2

        K0_BANK = (0, 3)

        F0_EARLY = {3: (F0_R, F0_A), 4: (F0_A + 1, F0_A + 2), 5: (F0_A + 3,), 6: (F0_Y, F0_Y + 1), 7: (F0_Y + 2, F0_Y + 3)}

        def l1_items(g, j, last):
            if last:
                return [(l1e_c, 0, L1E[(j, w)], w) for w in "oqk" if (j, w) in L1E]
            return [(l1_c, g, 4 * j + k, w) for k, w in enumerate("oqkv")]

        def l1_dst(j, what, part):
            if what == "q":
                return w_q1[:, j % 2, part, :]
            if what == "k":
                return w_k1[:, j % 2, part, :]
            if what == "o":
                return w_o1[:, j % 2, part, :]
            return w_v1[:, part, j, :]

        def l1_src(g, j, what):
            n = 4 * g + j
            if what == "v":
                return l1_v[bass.ds(g + 1, 1), j].rearrange("a p n -> (a p) n")
            w, k = {"q": (l1_q, n + 2), "k": (l1_k, n + 2), "o": (l1_o, n)}[what]
            return w[k] if isinstance(k, int) else w[bass.ds(k, 1)].rearrange("a p n -> (a p) n")

        def l1_free(eng, g, j, what):
            if what == "q":
                eng.wait_ge(k1_mm, 8 * g + 2 * j + 2)
            if what == "o" and not (isinstance(g, int) and g == 0 and j < 2):
                eng.wait_ge(o1_mm, 16 * g + 8 * (j // 2))
            if what == "v" and j == 0:
                eng.wait_ge(v1_mm, 8 * g + 8)

        def groups(eng, body):
            body(0, True, False)
            with eng.Fori(1, GROUPS - 1) as g:
                body(g, False, False)
            body(GROUPS - 1, False, True)

        def tiles(eng, body):
            for t in range(3):
                body(t, t % 2)
            with eng.Fori(1, (HT - 3) // 2) as i:
                body(i * 2 + 1, 1)
                body(i * 2 + 2, 0)
            for t in range(HT - 2, HT + 1):
                body(t, t % 2)

        @block.sync
        def _(sp):
            for i in range(kv_c.n):
                if i < 4:
                    sp.dma_start(x[:, i, :], ctx_t[0, i]).then_inc(ctx_loaded[i], 16)
                load(sp, kv_c, 0, i, kv_src(i))
                if i == 11:
                    sp.wait_ge(ctx_low, 4)
                    for b in range(NB):
                        sp.dma_start(x[:, b, :], x_in[b]).then_inc(x_loaded, 16)
            for i in range(4):
                load(sp, q0_c, 0, i, l0_q[0, i])

            def group(g, first, last):
                for b in range(NB):
                    for chunks, t, i, what, piece in l0_items(g, b, last):
                        if what == "o":
                            h = GH * g + piece
                            src = l0_o[h] if isinstance(h, int) else l0_o[bass.ds(h, 1)].rearrange("a p n -> (a p) n")
                        else:
                            src = l0_q[g + 1, piece] if isinstance(g, int) else l0_q[bass.ds(g + 1, 1), piece].rearrange("a p n -> (a p) n")
                        load(sp, chunks, t, i, src)
            groups(sp, group)
            for i in range(f0_c.n):
                load(sp, f0_c, 0, i, f0_src(i))
                if i == F0_K:
                    sp.wait_ge(o_mm, 64)
                    sp.dma_start(lnw[:, :], ln_w.partition_broadcast(P)).then_inc(lnw_loaded, 16)
            sp.wait_ge(ln_sems[2]["tr"], NB)
            for h in range(2):
                sp.dma_start(b_sb[:, h, :], bias[h]).then_inc(bias_loaded[h], 16)

            def group1(g, first, last):
                for j in range(GH):
                    for chunks, t, i, what in l1_items(g, j, last):
                        load(sp, chunks, t, i, l1_src(g, j, what))
                    if not (last and j >= 2):
                        n = 4 * g + j
                        src = bias[n + 2] if isinstance(n, int) else bias[bass.ds(n + 2, 1)].rearrange("a p n -> (a p) n")
                        sp.wait_ge(s1_biased, 2 * n + 2)
                        sp.dma_start(b_sb[:, j % 2, :], src).then_inc(bias_loaded[j % 2], 16)
            groups(sp, group1)
            sp.wait_ge(k1_mm, 2 * H)
            sp.wait_ge(v1_mm, NB * GROUPS)
            def packed(t, first=False):
                for k, (p, s_) in enumerate(((f1_p1, f1_s1), (f1_p3, f1_s3), (f1_p2, f1_s2))):
                    if not first:
                        sp.wait_ge(scaled, 3 * (t - 1) + k + 1)
                    for dst, src in ((pk, p), (ps, s_)):
                        at = src[t] if isinstance(t, int) else src[bass.ds(t, 1)].rearrange("a p n -> (a p) n")
                        sp.dma_start(dst[:, k, :], at).then_inc(pk_loaded[k], 16)

            packed(0, True)
            with sp.Fori(1, HT) as t:
                packed(t)
            for b in range(NB):
                sp.wait_ge(f1_added, NB * (HT - 1) + b + 1)
                sp.dma_start(out[b], x[:, b, :]).then_inc(stored, 16)
            sp.wait_ge(stored, 16 * NB)

        @block.gpsimd
        def _(pool):
            pool.memset(minus_half[:, :], -0.5).then_inc(ones_set, 1)
            pool.memset(ident[:, :], 0.0).then_inc(ident_set, 1)
            pool.wait_ge(ident_set, 1)
            pool.affine_select(out=ident[:, :], in_=ident[:, :], compare_op=ALU.not_equal, fill=1.0, base=0,
                               pattern=[[-1, P]], channel_multiplier=1).then_inc(ident_set, 1)
            pool.wait_ge(ones_set, 1)

            def kv_low(c):
                if kv_c.pattern[c] == "P":
                    low(pool, kv_c, 0, c, kv_dst(c, 1), kv_dst(c, 0))

            for c in range(6):
                kv_low(c)
            for i in range(24):
                if i < 16:
                    pool.wait_ge(k_eps, i + 1)
                    if i >= 1:
                        pool.wait_ge(k_hat, i)
                    pool.tensor_tensor(sc0[:, 2, :], sc0[:, 1, :], minus_half[:, 0:GH], ALU.pow).then_inc(k_rstd, 1)
                if i in KV_AHEAD:
                    kv_low(KV_AHEAD[i])
                if i in (12, 16):
                    ln_rstd(pool, 0, i // 4 - 3)
            for c in range(4):
                if q0_c.pattern[c] == "P":
                    low(pool, q0_c, 0, c, wq_slot(0, 1, c), wq_slot(0, 0, c))

            def square(s, b):
                pool.wait_ge(q_out, s + 1)
                if not (isinstance(s, int) and s == 0):
                    pool.wait_ge(q_sum, s)
                pool.tensor_tensor(q_sq[:, :], q_raw[:, b % 2, :], q_raw[:, b % 2, :], ALU.mult).then_inc(q_squared, 1)

            def normalise(s, b):
                pool.wait_ge(q_eps, s + 1)
                if not (isinstance(s, int) and s == 0):
                    pool.wait_ge(q_hat, s)
                pool.tensor_tensor(sc0[:, 4, :], sc0[:, 3, :], minus_half[:, 0:GH], ALU.pow).then_inc(q_rstd, 1)
                pool.wait_ge(q_rstd, s + 1)
                q = heads4(q_raw[:, b % 2, :])
                pool.tensor_tensor(q, q, over(sc0[:, 4, :], P), ALU.mult).then_inc(q_hat, 1)

            square(0, 0)
            normalise(0, 0)
            square(1, 1)

            def group(g, first, last):
                for b in range(NB):
                    s = NB * g + b
                    if not (last and b == 7):
                        normalise(s + 1, b + 1)
                    if not (last and b >= 6):
                        square(s + 2, b)
                    for chunks, t, i, what, piece in l0_items(g, b, last):
                        if chunks.pattern[i] == "P":
                            low(pool, chunks, t, i, l0_dst(g, what, piece, 1), l0_dst(g, what, piece, 0))
                    if last:
                        if b == 6:
                            ln_rstd(pool, 1, 0)
                        for i in F0_EARLY.get(b, ()):
                            low(pool, f0_c, 0, i, f0_dst(i, 1), f0_dst(i, 0))
            groups(pool, group)

            def low0(first, last):
                for i in range(first, last):
                    low(pool, f0_c, 0, i, f0_dst(i, 1), f0_dst(i, 0))

            ln_rstd(pool, 1, 1)
            low0(F0_B, F0_Q)

            def rms(f):
                pool.wait_ge(ln2_eps, f + 1)
                pool.tensor_tensor(rr[:, 4 * f:4 * f + 4], ve2[:, 4 * f:4 * f + 4], minus_half[:, 0:4], ALU.pow).then_inc(ln2_rr, 1)

            def residual(f):
                for b in range(4 * f, 4 * f + 4):
                    pool.wait_ge(ln_sems[2]["xn"], b + 1)
                    pool.tensor_tensor(x[:, b, :], x[:, b, :], xn[:, b % 2, :], ALU.add).then_inc(ln2_res, 1)

            ln_rstd(pool, 2, 0)
            rms(0)
            ln_rstd(pool, 2, 1)
            residual(0)
            low0(F0_Q, F0_Q1)
            rms(1)
            residual(1)
            low0(F0_Q1, F0_N)

            def group1(g, first, last):
                for j in range(GH):
                    for chunks, t, i, what in l1_items(g, j, last):
                        low(pool, chunks, t, i, l1_dst(j, what, 1), l1_dst(j, what, 0))
            groups(pool, group1)
            def low1(t, par, k, dst):
                pool.wait_ge(f1_high, 3 * t + k + 1)
                pool.tensor_tensor(dst[:, par, 1, :], dq[:, k, :], dst[:, par, 0, :].bitcast(F32), ALU.subtract).then_inc(f1_low, 1)

            low1(0, 0, 0, w_g)
            low1(0, 0, 1, w_u)
            ln_rstd(pool, 3, 0)
            ln_rstd(pool, 3, 1)
            low1(0, 0, 2, w_d)

            def tile(t, par):
                if isinstance(t, int) and t + 1 >= HT:
                    return
                for k, w in enumerate((w_g, w_u, w_d)):
                    low1(t + 1, 1 - par, k, w)

            tiles(pool, tile)

        @block.scalar
        def _(act):
            act.wait_ge(ones_set, 1)
            act.activation(ve2[:, 0:1], minus_half[:, 0:1], ACT.Copy)

            def kv_high(i):
                kv_free(act, i)
                high(act, kv_c, 0, i, kv_dst(i, 0))

            for i in range(6):
                if i < 4:
                    act.wait_ge(ctx_loaded[i], 16)
                    act.activation(wide[:, 0, i, 0:HALF], x[:, i, :], ACT.Copy).then_inc(ctx_high, 1)
                kv_high(i)
                if i == 3:
                    for dst, src in ((m0[:, :], mask0), (qn_w[:, :], q_norm), (kn_w[:, :], k_norm), (m1u[:, :, :], mask1),
                                     (shl[:, :], shift_l), (shr[:, :], shift_r), (keys[:, :], f0_keys)):
                        act.dma_start(dst, src).then_inc(small_loaded, 16)

            def q_evac(s, b):
                act.wait_ge(q_mm, s + 1)
                if not (isinstance(s, int) and s < 2):
                    act.wait_ge(qt_mm, s - 1)
                act.activation(q_raw[:, b % 2, :], bank[:, 0, :], ACT.Copy).then_inc(q_out, 1)

            for i in range(32):
                m, b = i // 8, i % 8
                act.wait_ge(kv_mm, i + 1)
                if m < 2:
                    if i >= 4:
                        act.wait_ge(kt_mm, i - 3)
                    act.activation(k_raw[:, i % 4, :], bank[:, i % 2, :], ACT.Copy)
                    if i >= 1:
                        act.wait_ge(k_sum, i)
                    act.activation(k_sq[:, :], bank[:, i % 2, :], ACT.Square).then_inc(kv_out, 1)
                else:
                    act.activation(v0[:, b, (m - 2) * D:(m - 1) * D], bank[:, kv_bank(i), :], ACT.Copy).then_inc(kv_out, 1)
                if i in KV_AHEAD:
                    kv_high(KV_AHEAD[i])
                if 17 <= i < 17 + NB:
                    ln_apply(act, 0, i - 17)
                if 19 <= i < 19 + NB:
                    ln_high(act, 0, i - 19)
                if i == 28:
                    for c in range(4):
                        high(act, q0_c, 0, c, wq_slot(0, 0, c))
                if i in (29, 30):
                    q_evac(i - 29, i - 29)

            def pt_evac(s):
                act.wait_ge(pt_mm, s + 1)
                if not (isinstance(s, int) and s == 0):
                    act.wait_ge(pv_mm, s)
                act.activation(p_t0[:, 0, :], bank[:, 3, :], ACT.Copy).then_inc(pt_out, 1)

            def ot_evac(s, b):
                act.wait_ge(pv_mm, s + 1)
                if not (isinstance(s, int) and s < 2):
                    act.wait_ge(o_mm, s - 1)
                act.activation(o_t0[:, b % 2, 0, :], bank[:, 5, :], ACT.Copy).then_inc(ot_high, 1)

            def high0(i):
                f0_free(act, i)
                high(act, f0_c, 0, i, f0_dst(i, 0))

            def w_highs(g, b, items):
                for chunks, t, i, what, piece in items:
                    l0_free(act, g, b, what, piece)
                    high(act, chunks, t, i, l0_dst(g, what, piece, 0))

            def group(g, first, last):
                for b in range(NB):
                    s = NB * g + b
                    head = first and b == 0
                    if not head:
                        pt_evac(s - 1)
                    items = l0_items(g, b, last)
                    if b == 2:
                        w_highs(g, b, items)
                    act.wait_ge(s_max, s + 1)
                    if not head:
                        act.wait_ge(pt_mm, s)
                    for h in range(GH):
                        e = act.activation(p0[:, h, :], sm0[:, h, :], ACT.Exp, bias=sc0[:, 5, h:h + 1], accum_out=sc0[:, 6, h:h + 1])
                    e.then_inc(p_exp, 1)
                    if not (last and b >= 6):
                        q_evac(s + 2, b)
                    if not head:
                        ot_evac(s - 1, b + 1)
                    if b != 2:
                        w_highs(g, b, items)
                    if last:
                        for i in F0_EARLY.get(b, ()):
                            high0(i)
                        if b == 7:
                            ln_apply(act, 1, 0)
                            ln_apply(act, 1, 1)
            groups(act, group)
            s = NB * GROUPS
            pt_evac(s - 1)
            ln_high(act, 1, 0)
            ln_apply(act, 1, 2)
            ln_high(act, 1, 1)
            ln_apply(act, 1, 3)
            ot_evac(s - 1, 1)
            ln_high(act, 1, 2)
            ln_high(act, 1, 3)
            def r_evac(f):
                act.wait_ge(r_mm, f + 1)
                act.activation(qr[:, f * HALF:(f + 1) * HALF], bank[0:RD, 3, :], ACT.Copy).then_inc(r_out, 1)

            def z_evac(b):
                act.wait_ge(z_mm, b + 1)
                act.activation(z[:, b, :], bank[:, b % 2, :], ACT.Copy).then_inc(z_out, 1)

            ln_apply(act, 1, 4)
            ln_apply(act, 1, 5)
            r_evac(0)
            z_evac(0)
            z_evac(1)
            for b in (4, 5):
                ln_high(act, 1, b)
                ln_apply(act, 1, b + 2)
                z_evac(b - 2)
                high0(F0_B + b - 4)
            ln_high(act, 1, 6)
            ln_high(act, 1, 7)
            high0(F0_B + 2)
            high0(F0_B + 3)
            r_evac(1)
            high0(F0_K)
            for b in range(4, NB):
                z_evac(b)
                high0(F0_V + b - 4)
                if b == 5:
                    act.wait_ge(sub_done, 1)
                    act.activation(gate[:, :, :], gate[:, :, :], ACT.Exp).then_inc(exp_done, 1)

            def k_evac0(f):
                act.wait_ge(k1_mm, 2 - f)
                act.activation(k_t1[:, 0, f * HALF:(f + 1) * HALF], bank[:, K0_BANK[f], :], ACT.Copy).then_inc(k1_out, 1)

            def v_evac0(k):
                act.wait_ge(v1_mm, k + 1)
                act.activation(v1[:, V_ORDER[k], :], bank[:, v0_bank(k), :], ACT.Copy).then_inc(v1_out, 1)

            k_evac0(1)
            for b in range(NB):
                act.wait_ge(zt_mm, b + 1)
                if b >= 2:
                    act.wait_ge(f0_mm, b - 1)
                act.activation(z_t[:, b % 2, 0, :], bank[:, 4 + b % 2, :], ACT.Copy).then_inc(zt_high, 1)
                if b == 1:
                    v_evac0(0)
                if 1 <= b < 5:
                    high0(F0_X + b - 1)

            def squares(f):
                act.wait_ge(ln_sems[2]["nmr"], f + 1)
                for b in range(4 * f, 4 * f + 4):
                    if b >= 1:
                        act.wait_ge(ln2_ss, b)
                    act.activation(rep1[:, :, :].rearrange("p b e -> p (b e)"), x[:, b, :], ACT.Square, bias=nmr[:, b:b + 1],
                                   scale=rs[:, b:b + 1], accum_out=hs[:, b:b + 1]).then_inc(ln2_ss, 1)

            def apply2(b):
                if b >= 2:
                    act.wait_ge(ln2_res, b - 1)
                    act.wait_ge(ln2_w, b - 1)
                ln_apply(act, 2, b)

            def qk_evac(n, j, k):
                act.wait_ge(q1_mm if k < 2 else k1_mm, 2 * n + k % 2 + 1)
                dst = (q_t1 if k < 2 else k_t1)[:, j % 2, (k % 2) * HALF:(k % 2 + 1) * HALF]
                act.activation(dst, bank[:, k % 2, :], ACT.Copy).then_inc(q1_out if k < 2 else k1_out, 1)

            def v_evac(g, b):
                act.wait_ge(v1_mm, 8 * g + b + 1)
                act.activation(v1[:, b, :], bank[:, 6 + b % 2, :], ACT.Copy).then_inc(v1_out, 1)

            squares(0)
            apply2(0)
            apply2(1)
            v_evac0(1)
            v_evac0(2)
            ln_high(act, 2, 0)
            apply2(2)
            v_evac0(3)
            ln_high(act, 2, 1)
            apply2(3)
            k_evac0(0)
            ln_high(act, 2, 2)
            v_evac0(4)
            ln_high(act, 2, 3)
            high0(F0_Q)
            squares(1)
            v_evac0(5)
            apply2(4)
            apply2(5)
            v_evac0(6)
            ln_high(act, 2, 4)
            apply2(6)
            ln_high(act, 2, 5)
            apply2(7)
            qk_evac(0, 0, 0)
            ln_high(act, 2, 6)
            ln_high(act, 2, 7)
            v_evac0(7)
            high0(F0_Q1)
            high0(F0_K1)
            qk_evac(0, 0, 1)

            def group1(g, first, last):
                for j in range(GH):
                    n = 4 * g + j
                    head0 = first and j == 0
                    end = last and j == GH - 1
                    items = l1_items(g, j, last)

                    def item(k):
                        if k < len(items):
                            chunks, t, i, what = items[k]
                            l1_free(act, g, j, what)
                            high(act, chunks, t, i, l1_dst(j, what, 0))

                    for f in range(2):
                        act.wait_ge(s1_floor, 2 * n + f + 1)
                        if not head0:
                            act.wait_ge(pt1_mm, 2 * n - 1 + f)
                        for b in range(4):
                            e = act.activation(p1[:, f, b, :], sm1[:, f, b, :], ACT.Exp, bias=nmx1[:, f, b:b + 1],
                                               accum_out=sum1[:, f, b:b + 1])
                        e.then_inc(p1_exp, 1)
                        if not end:
                            qk_evac(n + 1, j + 1, f)
                        if f == 1:
                            item(0)
                    for f in range(2):
                        act.wait_ge(pt1_mm, 2 * n + f + 1)
                        if not head0:
                            act.wait_ge(pv1_mm, 2 * n - 1 + f)
                        act.activation(p_t1[:, f, :], bank[:, 4, :], ACT.Copy).then_inc(pt1_out, 1)
                        if not end:
                            qk_evac(n + 1, j + 1, 2 + f)
                        act.wait_ge(pv1_mm, 2 * n + f + 1)
                        if not (first and j < 2):
                            act.wait_ge(o1_mm, 16 * g + 8 * (j // 2))
                        act.activation(o_t1[:, j % 2, 0, f * HALF:(f + 1) * HALF], bank[:, 5, :], ACT.Copy).then_inc(ot1_high, 1)
                        if f == 0:
                            item(1)
                    item(2)
                    item(3)
                    if j == GH - 1 and not last:
                        for b in range(NB):
                            v_evac(g + 1, b)
            groups(act, group1)

            def high1(t, par, k, dst, reused=True):
                act.wait_ge(scaled, 3 * t + k + 1)
                if reused:
                    if k < 2:
                        act.wait_ge(ab_mm, 4 * t - 4)
                    else:
                        act.wait_ge(f1_mm, NB * t - NB)
                act.activation(dst[:, par, 0, :], dq[:, k, :], ACT.Copy).then_inc(f1_high, 1)

            def silu(t, f, first):
                act.wait_ge(ab_mm, 4 * t + 2 * f + 2)
                if not first:
                    act.wait_ge(h_done, 2 * t + f - 1)
                act.activation(sl[:, f, :], bank[:, 2 * f, :], ACT.Silu).then_inc(silu_done, 1)

            def h_split(t, par, f, reused):
                act.wait_ge(h_done, 2 * t + f + 1)
                if reused:
                    act.wait_ge(f1_mm, NB * t - NB)
                act.activation(h_t[:, par, 0, f * HALF:(f + 1) * HALF], hf[:, f, :], ACT.Copy).then_inc(h_high, 1)

            high1(0, 0, 0, w_g, False)
            act.wait_ge(s1_mm, 2 * H)
            high1(0, 0, 1, w_u, False)
            ln_apply(act, 3, 0)
            ln_apply(act, 3, 1)
            ln_high(act, 3, 0)
            ln_apply(act, 3, 2)
            ln_high(act, 3, 1)
            ln_apply(act, 3, 3)
            ln_high(act, 3, 2)
            ln_high(act, 3, 3)
            ln_apply(act, 3, 4)
            ln_apply(act, 3, 5)
            act.wait_ge(o1_mm, 4 * H)
            high1(0, 0, 2, w_d, False)
            for b in range(6, NB):
                ln_high(act, 3, b - 2)
                ln_apply(act, 3, b)
            ln_high(act, 3, 6)
            ln_high(act, 3, 7)
            high1(1, 1, 0, w_g, False)
            high1(1, 1, 1, w_u, False)

            def tile(t, par):
                first = isinstance(t, int) and t == 0
                end = t if isinstance(t, int) else 0
                for f in range(2 if end < HT else 0):
                    silu(t, f, first)
                    h_split(t, par, f, not (isinstance(t, int) and t < 2) )
                    if f == 0 and end + 1 < HT:
                        high1(t + 1, 1 - par, 2, w_d, not first)
                if end + 2 < HT:
                    high1(t + 2, par, 0, w_g)
                    high1(t + 2, par, 1, w_u)
            tiles(act, tile)

        @block.vector
        def _(dve):
            def lows(chunks, t, i, dst):
                if chunks.pattern[i] == "D":
                    low(dve, chunks, t, i, dst(1), dst(0))

            for i in range(6):
                if i < 4:
                    dve.wait_ge(ctx_high, i + 1)
                    dve.tensor_tensor(wide[:, 1, i, 0:HALF], x[:, i, :], wide[:, 0, i, 0:HALF].bitcast(F32), ALU.subtract).then_inc(ctx_low, 1)
                lows(kv_c, 0, i, lambda q: kv_dst(i, q))
            dve.wait_ge(small_loaded, 16 * 7)
            dve.scalar_tensor_tensor(qk_w[:, :], qn_w[:, :], float(P) ** 0.5, kn_w[:, :], ALU.mult, ALU.mult).then_inc(qk_w_set, 1)
            dve.wait_ge(qk_w_set, 1)
            for i in range(20):
                if i < 16:
                    dve.wait_ge(kv_out, i + 1)
                    if i >= 1:
                        dve.wait_ge(k_eps, i)
                    dve.tensor_reduce(sc0[:, 0, :], heads4(k_sq[:, :]), AX.X, ALU.add).then_inc(k_sum, 1)
                    dve.wait_ge(k_sum, i + 1)
                    if i >= 1:
                        dve.wait_ge(k_rstd, i)
                    dve.tensor_scalar(sc0[:, 1, :], sc0[:, 0, :], EPS * P, None, ALU.add).then_inc(k_eps, 1)
                if 1 <= i < 17:
                    k = i - 1
                    dve.wait_ge(k_rstd, k + 1)
                    kr = heads4(k_raw[:, k % 4, :])
                    dve.tensor_tensor(kr, kr, over(sc0[:, 2, :], P), ALU.mult).then_inc(k_hat, 1)
                if 3 <= i < 19:
                    k = i - 3
                    m, b = k // 8, k % 8
                    dve.wait_ge(kt_mm, k + 1)
                    dst = k_t[:, :].rearrange("p (g t) -> p g t", g=KVH)[:, 4 * m:4 * m + 4, b * P:(b + 1) * P]
                    dve.tensor_scalar(dst, heads4(bank[:, 2 + k % 2, :]), qk_w[:, 0:1], None, ALU.mult).then_inc(kt_out, 1)
                if i == 8:
                    dve.wait_ge(x_loaded, 16 * NB)
                if 8 <= i < 8 + NB:
                    ln_stats(dve, 0, i - 8)
                if i in (14, 18):
                    ln_nmr(dve, 0, (i - 14) // 4)

            for b in range(NB):
                ln_low(dve, 0, b)
            for c in range(4):
                lows(q0_c, 0, c, lambda q: wq_slot(0, q, c))

            def q_sums(s):
                dve.wait_ge(q_squared, s + 1)
                if not (isinstance(s, int) and s == 0):
                    dve.wait_ge(q_eps, s)
                dve.tensor_reduce(sc0[:, 7, :], heads4(q_sq[:, :]), AX.X, ALU.add).then_inc(q_sum, 1)
                dve.wait_ge(q_sum, s + 1)
                if not (isinstance(s, int) and s == 0):
                    dve.wait_ge(q_rstd, s)
                dve.tensor_scalar(sc0[:, 3, :], sc0[:, 7, :], EPS * P, None, ALU.add).then_inc(q_eps, 1)

            def qt_evac(s):
                dve.wait_ge(qt_mm, s + 1)
                if not (isinstance(s, int) and s == 0):
                    dve.wait_ge(s_mm, s)
                dve.tensor_copy(q_t[:, :], bank[:, 2, :]).then_inc(qt_out, 1)

            q_sums(0)
            q_sums(1)
            qt_evac(0)

            dve.wait_ge(kv_out, 32)

            def add_x(s, b):
                dve.wait_ge(o_mm, s + 1)
                dve.tensor_tensor(x[:, b % NB, :], bank[:, 1, :], x[:, b % NB, :], ALU.add).then_inc(x_added, 1)

            def pt_lo(s):
                dve.wait_ge(pt_out, s + 1)
                dve.tensor_tensor(p_t0[:, 1, :], bank[:, 3, :], p_t0[:, 0, :].bitcast(F32), ALU.subtract).then_inc(pt_low, 1)

            def ot_lo(s, b):
                dve.wait_ge(ot_high, s + 1)
                dve.tensor_tensor(o_t0[:, b % 2, 1, :], bank[:, 5, :], o_t0[:, b % 2, 0, :].bitcast(F32), ALU.subtract).then_inc(ot_low, 1)

            def w_lows(g, b, last):
                for chunks, t, i, what, piece in l0_items(g, b, last):
                    if chunks.pattern[i] == "D":
                        low(dve, chunks, t, i, l0_dst(g, what, piece, 1), l0_dst(g, what, piece, 0))

            def group(g, first, last):
                for b in range(NB):
                    s = NB * g + b
                    head = first and b == 0
                    dve.wait_ge(s_mm, s + 1)
                    if not head:
                        dve.wait_ge(p_exp, s)
                    dve.tensor_tensor(sm0[:, :, :], heads4(bank[:, 4, :]), repeat(m0[:, :], GH), ALU.add).then_inc(s_masked, 1)
                    dve.wait_ge(s_masked, s + 1)
                    dve.tensor_reduce(sc0[:, 5, :], sm0[:, :, :], AX.X, ALU.max, negate=True).then_inc(s_max, 1)
                    if not (first and b < 2):
                        dve.wait_ge(pv_mm, s - 1)
                    src = v0[:, b, g * P:(g + 1) * P] if isinstance(g, int) else v0[:, b, bass.ds(g * P, P)]
                    dve.tensor_copy(v_st[:, b % 2, 0, :], src).then_inc(v_high, 1)
                    if not head:
                        pt_lo(s - 1)
                    dve.wait_ge(v_high, s + 1)
                    dve.tensor_tensor(v_st[:, b % 2, 1, :], src, v_st[:, b % 2, 0, :].bitcast(F32), ALU.subtract).then_inc(v_staged, 1)
                    if not (first and b < 3):
                        if not (first and b == 3):
                            dve.wait_ge(x_added, s - 3)
                        add_x(s - 3, b - 3)
                    if b == 2:
                        w_lows(g, 1, last)
                        w_lows(g, 2, last)
                    if last and b >= 3:
                        dve.wait_ge(x_added, s - 2)
                        ln_stats(dve, 1, b - 3)
                        if b == 7:
                            ln_nmr(dve, 1, 0)
                    dve.wait_ge(p_exp, s + 1)
                    if not head:
                        dve.wait_ge(p_norm, s)
                    dve.reciprocal(sc0[:, 0, :], sc0[:, 6, :]).then_inc(p_inv, 1)
                    dve.wait_ge(p_inv, s + 1)
                    dve.tensor_tensor(p0[:, :, :], p0[:, :, :], over(sc0[:, 0, :], P), ALU.mult).then_inc(p_norm, 1)
                    if not (last and b == 7):
                        qt_evac(s + 1)
                    if not head:
                        ot_lo(s - 1, b + 1)
                    if not (last and b >= 6):
                        q_sums(s + 2)
                    if b not in (1, 2):
                        w_lows(g, b, last)
            groups(dve, group)
            s = NB * GROUPS
            pt_lo(s - 1)
            ln_low(dve, 1, 0)
            ln_low(dve, 1, 1)

            def last_x(b):
                add_x(s - NB + b, b)
                dve.wait_ge(x_added, s - NB + b + 1)
                ln_stats(dve, 1, b)

            last_x(5)
            ot_lo(s - 1, 1)
            ln_low(dve, 1, 2)
            last_x(6)
            ln_low(dve, 1, 3)
            last_x(7)
            ln_nmr(dve, 1, 1)

            for b in range(4, NB):
                ln_low(dve, 1, b)
            dve.wait_ge(sc_mm, 1)
            dve.tensor_copy(scr[:, :, :], bank[:, 2, :].rearrange("p (b e) -> p b e", b=NB)).then_inc(sc_out, 1)
            dve.wait_ge(sc_out, 1)
            for b in range(NB):
                dve.max(top1[:, b, :], scr[:, b, :]).then_inc(t1_done, 1)
            for b in range(NB):
                dve.wait_ge(t1_done, b + 1)
                dve.match_replace(rep1[:, b, :], top1[:, b, :], scr[:, b, :], MASKED).then_inc(rep1_done, 1)
            dve.tensor_tensor(gate[:, :, :], scr[:, :, :], top1[:, :, 0:1].broadcast_to([P, NB, NE]), ALU.subtract).then_inc(sub_done, 1)
            for b in range(NB):
                dve.wait_ge(rep1_done, b + 1)
                dve.max(top2[:, b, :], rep1[:, b, :]).then_inc(t2_done, 1)
            for b in range(NB):
                dve.wait_ge(t2_done, b + 1)
                dve.match_replace(rep2[:, b, :], top2[:, b, :], rep1[:, b, :], MASKED).then_inc(rep2_done, 1)
            dve.wait_ge(rep2_done, NB)
            dve.tensor_tensor(rep2[:, :, :], rep2[:, :, :], scr[:, :, :], ALU.not_equal).then_inc(sel_done, 1)
            dve.wait_ge(sel_done, 1)
            dve.wait_ge(exp_done, 1)
            dve.tensor_tensor(gate[:, :, :], gate[:, :, :], rep2[:, :, :], ALU.mult).then_inc(gated, 1)
            dve.wait_ge(gated, 1)
            dve.tensor_reduce(gsum[:, :], gate[:, :, :], AX.X, ALU.add).then_inc(g_sum, 1)
            dve.wait_ge(g_sum, 1)
            dve.reciprocal(ginv[:, :], gsum[:, :]).then_inc(g_inv, 1)
            dve.wait_ge(g_inv, 1)
            dve.tensor_tensor(gate[:, :, :], gate[:, :, :], over(ginv[:, :], NE), ALU.mult).then_inc(g_done, 1)
            dve.wait_ge(g_done, 1)

            def gate_z(b):
                dve.wait_ge(z_out, b + 1)
                zb = z[:, b, :].rearrange("p (e r) -> p e r", e=NE)
                dve.tensor_tensor(zb, zb, over(gate[:, b, :], RANK), ALU.mult).then_inc(z_gated, 1)

            def zt_lo(b):
                dve.wait_ge(zt_high, b + 1)
                dve.tensor_tensor(z_t[:, b % 2, 1, :], bank[:, 4 + b % 2, :], z_t[:, b % 2, 0, :].bitcast(F32), ALU.subtract).then_inc(zt_low, 1)

            gate_z(0)
            gate_z(1)
            gate_z(2)
            zt_lo(0)
            for b in range(NB):
                if b + 1 < NB:
                    zt_lo(b + 1)
                if b + 3 < NB:
                    gate_z(b + 3)
                dve.wait_ge(f0_mm, b + 1)
                dve.scalar_tensor_tensor(x[:, b, :], bank[:, 6 + b % 2, :], 2.0, x[:, b, :], ALU.mult, ALU.add).then_inc(f0_added, 1)
                dve.wait_ge(f0_added, b + 1)
                ln_stats(dve, 2, b)
                if b == 5:
                    ln_nmr(dve, 2, 0)

            def rms(f):
                dve.wait_ge(ln2_ss, 4 * f + 4)
                dve.tensor_scalar(ve2[:, 4 * f:4 * f + 4], hs[:, 4 * f:4 * f + 4], 1.0 / D, EPS, ALU.mult, ALU.add).then_inc(ln2_eps, 1)

            def weighted(b):
                dve.wait_ge(ln_sems[2]["xn"], b + 1)
                dve.wait_ge(ln2_rr, b // 4 + 1)
                if b >= 2:
                    dve.wait_ge(ln_sems[2]["tr"], b - 1)
                dve.scalar_tensor_tensor(xw2[:, b % 2, :], xn[:, b % 2, :], rr[:, b:b + 1], lnw[:, :], ALU.mult, ALU.mult).then_inc(ln2_w, 1)

            rms(0)
            dve.wait_ge(lnw_loaded, 16)
            weighted(0)
            weighted(1)
            ln_nmr(dve, 2, 1)
            for b in range(4):
                ln_low(dve, 2, b)
                if b < 2:
                    weighted(b + 2)
            rms(1)
            weighted(4)
            weighted(5)
            for b in range(4, NB):
                ln_low(dve, 2, b)
                if b < 6:
                    weighted(b + 2)

            def unpack(t, k, first=False):
                dve.wait_ge(pk_loaded[k], 32 * (t + 1))
                if not first:
                    dve.wait_ge(scaled, 3 * t + k - 2)
                if k < 2:
                    dve.tensor_scalar(sh[:, k, :], pk[:, k, :], shl[:, 0:1], shr[:, 0:1], ALU.logical_shift_left,
                                      ALU.arith_shift_right).then_inc(unpacked, 1)
                else:
                    for c in range(4):
                        a = sh[:, k, :].rearrange("p (a c) -> p a c", c=4)[:, :, c]
                        i = pk[:, k, :].rearrange("p (a c) -> p a c", c=4)[:, :, c]
                        u = dve.tensor_scalar(a, i, shl[:, c:c + 1], shr[:, c:c + 1], ALU.logical_shift_left, ALU.arith_shift_right)
                    u.then_inc(unpacked, 1)

            def scale(t, k, first=False):
                u = 3 * t + k
                dve.wait_ge(unpacked, u + 1)
                if not first:
                    dve.wait_ge(f1_low, u - 2)
                dve.tensor_tensor(dq[:, k, :], sh[:, k, :], ps[:, k, :], ALU.mult).then_inc(scaled, 1)

            dve.wait_ge(zt_mm, NB)
            dve.tensor_scalar(m1[:, :, :], m1u[:, :, :], -1.0, -MASKED, ALU.add, ALU.mult).then_inc(mask_set, 1)
            dve.wait_ge(mask_set, 1)

            def group1(g, first, last):
                for j in range(GH):
                    n = 4 * g + j
                    head0 = first and j == 0
                    par = j % 2
                    for f in range(2):
                        k = 2 * n + f
                        dve.wait_ge(s1_mm, k + 1)
                        if f == 0:
                            dve.wait_ge(bias_loaded[par], 16 * ((GH // 2) * g + j // 2 + 1))
                        if not head0:
                            dve.wait_ge(p1_exp, k - 1)
                        dve.tensor_tensor(sm1[:, f], bank[:, 2 + f, :].rearrange("p (b n) -> p b n", b=4), repeat(b_sb[:, par, :], 4),
                                          ALU.add).then_inc(s1_biased, 1)
                        dve.wait_ge(s1_biased, k + 1)
                        dve.tensor_tensor(sm1[:, f], sm1[:, f], m1[:, 4 * f:4 * f + 4, :], ALU.add).then_inc(s1_masked, 1)
                        dve.wait_ge(s1_masked, k + 1)
                        dve.tensor_reduce(nmx1[:, f], sm1[:, f], AX.X, ALU.max, negate=True).then_inc(s1_max, 1)
                        dve.wait_ge(s1_max, k + 1)
                        dve.tensor_scalar(nmx1[:, f], nmx1[:, f], -MAX_FLOOR, None, ALU.min).then_inc(s1_floor, 1)
                    for f in range(2):
                        k = 2 * n + f
                        dve.wait_ge(p1_exp, k + 1)
                        dve.tensor_scalar(inv1[:, f], sum1[:, f], 1e-30, None, ALU.max).then_inc(p1_guard, 1)
                        dve.wait_ge(p1_guard, k + 1)
                        dve.reciprocal(inv1[:, f], inv1[:, f]).then_inc(p1_inv, 1)
                        dve.wait_ge(p1_inv, k + 1)
                        dve.tensor_tensor(p1[:, f], p1[:, f], over(inv1[:, f], P), ALU.mult).then_inc(p1_norm, 1)
                    end = last and j == 3

                    def ot1_lo(f):
                        dve.wait_ge(ot1_high, 2 * n + f + 1)
                        dve.tensor_tensor(o_t1[:, par, 1, f * HALF:(f + 1) * HALF], bank[:, 5, :],
                                          o_t1[:, par, 0, f * HALF:(f + 1) * HALF].bitcast(F32), ALU.subtract).then_inc(ot1_low, 1)

                    if end:
                        for k in range(3):
                            unpack(0, k, True)
                        ot1_lo(0)
                        scale(0, 0, True)
                        scale(0, 1, True)
                    else:
                        ot1_lo(0)
                        ot1_lo(1)
                    for b in range(NB if j % 2 else 0):
                        u = 16 * g + 8 * (j // 2) + b
                        dve.wait_ge(o1_mm, u + 1)
                        if not (first and j == 1):
                            dve.wait_ge(x1_added, u - 7)
                        elif b == 0:
                            dve.wait_ge(ln2_res, NB)
                        src = LAST_BANKS[b] if end else 6 + b % 2
                        dve.tensor_tensor(x[:, b, :], bank[:, src, :], x[:, b, :], ALU.add).then_inc(x1_added, 1)
                        if end:
                            dve.wait_ge(x1_added, u + 1)
                            ln_stats(dve, 3, b)
                            if b == 1:
                                ot1_lo(1)
                            if b == 4:
                                ln_nmr(dve, 3, 0)
                            if b in (5, 6):
                                ln_low(dve, 3, 2 * b - 10)
                                ln_low(dve, 3, 2 * b - 9)
            groups(dve, group1)

            scale(0, 2, True)
            ln_nmr(dve, 3, 1)
            for k in range(3):
                unpack(1, k)
            for b in range(4, NB):
                ln_low(dve, 3, b)
            for k in range(3):
                scale(1, k)

            def tile(t, par):
                first = isinstance(t, int) and t == 0
                end = t if isinstance(t, int) else 1
                for f in range(2):
                    if end < HT:
                        dve.wait_ge(silu_done, 2 * t + f + 1)
                        if not first:
                            dve.wait_ge(h_low, 2 * t + f - 1)
                        dve.tensor_tensor(hf[:, f, :], bank[:, 2 * f + 1, :], sl[:, f, :], ALU.mult).then_inc(h_done, 1)
                        dve.wait_ge(h_high, 2 * t + f + 1)
                        dve.tensor_tensor(h_t[:, par, 1, f * HALF:(f + 1) * HALF], hf[:, f, :],
                                          h_t[:, par, 0, f * HALF:(f + 1) * HALF].bitcast(F32), ALU.subtract).then_inc(h_low, 1)
                    for b in range(4 * f, 4 * f + 4) if not first else ():
                        dve.wait_ge(f1_mm, NB * t - NB + b + 1)
                        if not (isinstance(t, int) and t == 1):
                            dve.wait_ge(f1_added, NB * t - 2 * NB + b + 1)
                        dve.tensor_tensor(x[:, b, :], bank[:, 4 + b % 4, :], x[:, b, :], ALU.add).then_inc(f1_added, 1)
                    if end + 2 < HT:
                        for k in range(3):
                            (scale if f else unpack)(t + 2, k)
            tiles(dve, tile)

        @block.tensor
        def _(pe):
            pe.wait_ge(ident_set, 2)
            def q_mms(s, b, par, before):
                if not (isinstance(s, int) and s == 0):
                    pe.wait_ge(q_out, s)
                product(pe, bank[:, 0, :], [(l, (wq_slot(par, 0, kt), wq_slot(par, 1, kt))) for kt, l in enumerate(xn_tile(b % NB))],
                        before=before).then_inc(q_mm, 1)

            def q_transposes(s, b):
                pe.wait_ge(q_hat, s + 1)
                if not (isinstance(s, int) and s == 0):
                    pe.wait_ge(qt_out, s)
                transposes(pe, 2, q_raw[:, b % 2, :]).then_inc(qt_mm, 1)

            for i in range(32):
                m, b = i // 8, i % 8
                before = None
                if i == 0:
                    def before(kt):
                        pe.wait_ge(ctx_low, kt + 1)
                        wait_low(pe, kv_c, 0, kt)
                elif i == 4:
                    before = lambda kt: wait_low(pe, kv_c, 0, 4 + kt)
                elif b == 0:
                    before = lambda kt: wait_low(pe, kv_c, 0, 4 + 4 * m + kt)
                if i >= 2:
                    pe.wait_ge(kv_out, i - 1)
                product(pe, bank[:, kv_bank(i), :], [(l, (kv_slot(m, 0, kt), kv_slot(m, 1, kt))) for kt, l in enumerate(ctx_tile(b))],
                        before=before).then_inc(kv_mm, 1)
                if 3 <= i < 19:
                    k = i - 3
                    pe.wait_ge(k_hat, k + 1)
                    if k >= 2:
                        pe.wait_ge(kt_out, k - 1)
                    transposes(pe, 2 + k % 2, k_raw[:, k % 4, :]).then_inc(kt_mm, 1)
                if 19 <= i < 19 + NB:
                    ln_transpose(pe, 0, i - 19)
                if i == 29:
                    pe.wait_ge(ln_sems[0]["low"], NB)
                    pe.wait_ge(kt_out, 16)
                    q_mms(0, 0, 0, lambda kt: wait_lows(pe, q0_c, 0, kt, kt))
                if i == 30:
                    q_mms(1, 1, 0, None)
                    q_transposes(0, 0)

            def pt(s):
                pe.wait_ge(p_norm, s + 1)
                if not (isinstance(s, int) and s == 0):
                    pe.wait_ge(pt_low, s)
                transposes(pe, 3, p0[:, :, :].rearrange("p h n -> p (h n)")).then_inc(pt_mm, 1)

            def pv(s, b):
                pe.wait_ge(v_staged, s + 1)
                pe.wait_ge(pt_low, s + 1)
                if not (isinstance(s, int) and s == 0):
                    pe.wait_ge(ot_low, s)
                product(pe, bank[:, 5, :], [((v_st[:, b % 2, 0, :], v_st[:, b % 2, 1, :]), (p_t0[:, 0, :], p_t0[:, 1, :]))]).then_inc(pv_mm, 1)

            def project(s, b, before=None):
                pe.wait_ge(ot_low, s + 1)
                if not (isinstance(s, int) and s == 0):
                    pe.wait_ge(x_added, s)
                product(pe, bank[:, 1, :], [((o_t0[:, b % 2, 0, h * P:(h + 1) * P], o_t0[:, b % 2, 1, h * P:(h + 1) * P]),
                                             (w_o0[:, 0, h, :], w_o0[:, 1, h, :])) for h in range(GH)], before=before).then_inc(o_mm, 1)

            def group(g, first, last):
                for b in range(NB):
                    s = NB * g + b
                    head = first and b == 0
                    pe.wait_ge(qt_out, s + 1)
                    if not head:
                        pe.wait_ge(s_masked, s)
                    at = g * TOK + b * P
                    rhs = k_t[:, at:at + P] if isinstance(at, int) else k_t[:, bass.ds(at, P)]
                    for h in range(GH):
                        mm = pe.matmul(bank[:, 4, h * P:(h + 1) * P], q_t[:, h * P:(h + 1) * P], rhs, start=True, stop=True)
                    mm.then_inc(s_mm, 1)
                    if not head:
                        pt(s - 1)
                    if not (last and b >= 6):
                        if b < 6:
                            q_mms(s + 2, b + 2, g % 2, None)
                        else:
                            need = (lambda kt: wait_lows(pe, l0_c, g, 4 + kt if kt else 0, 4 + kt if kt else 0)) if b == 6 else None
                            q_mms(s + 2, b + 2, (g + 1) % 2, need)
                    short = last and b >= 6
                    if not head and not short:
                        pv(s - 1, b + 1)
                    if not (last and b == 7):
                        q_transposes(s + 1, b + 1)
                    if short:
                        pv(s - 1, b + 1)
                    if not (first and b < 2):
                        if b == 2 and last:
                            project(s - 2, b, lambda h: wait_lows(pe, l0e_c, 0, h, h))
                        elif b == 2:
                            project(s - 2, b, lambda h: wait_lows(pe, l0_c, g, 1 + h, 1 + h))
                        else:
                            project(s - 2, b)
            groups(pe, group)
            s = NB * GROUPS
            pt(s - 1)
            ln_transpose(pe, 1, 0)
            ln_transpose(pe, 1, 1)
            pv(s - 1, 1)
            ln_transpose(pe, 1, 2)
            project(s - 2, 0)
            ln_transpose(pe, 1, 3)
            project(s - 1, 1)

            def router(f):
                pe.wait_ge(ln_sems[1]["low"], 4 * f + 4)
                if f == 0:
                    wait_lows(pe, f0_c, 0, F0_R, F0_R)
                else:
                    pe.wait_ge(r_out, 1)
                terms = [((w_r[:, 0, kt * P:(kt + 1) * P], w_r[:, 1, kt * P:(kt + 1) * P]), r) for kt, r in enumerate(xn_half(f))]
                product(pe, bank[:, 3, :], terms).then_inc(r_mm, 1)

            def experts(b):
                if b == 0:
                    wait_lows(pe, f0_c, 0, F0_A, F0_A + 3)
                elif b == 1:
                    pe.wait_ge(x_added, s)
                else:
                    pe.wait_ge(z_out, b - 1)
                pe.wait_ge(ln_sems[1]["low"], b + 1)
                product(pe, bank[:, b % 2, :], [(l, (wide[:, 0, kt, 0:D], wide[:, 1, kt, 0:D])) for kt, l in enumerate(xn_tile(b))]).then_inc(z_mm, 1)

            router(0)
            experts(0)
            experts(1)
            ln_transpose(pe, 1, 4)
            ln_transpose(pe, 1, 5)
            experts(2)
            ln_transpose(pe, 1, 6)
            experts(3)
            ln_transpose(pe, 1, 7)
            experts(4)
            router(1)
            pe.wait_ge(small_loaded, 16 * 7)
            for b in range(NB):
                pe.wait_ge(r_out, b // 4 + 1)
                mm = pe.matmul(bank[:, 2, b * NE:(b + 1) * NE], qr[:, b * P:(b + 1) * P], keys[:, :], start=True, stop=True)
            mm.then_inc(sc_mm, 1)
            for b in range(5, NB):
                experts(b)

            def w_head(w, par, kt):
                return w[:, par, 0, kt * P:(kt + 1) * P], w[:, par, 1, kt * P:(kt + 1) * P]

            def ctx_half(f):
                return [(wide[:, 0, kt, f * HALF:(f + 1) * HALF], wide[:, 1, kt, f * HALF:(f + 1) * HALF]) for kt in range(KT)]

            def k0(f):
                product(pe, bank[:, K0_BANK[f], :], [(w_head(w_k1, 0, kt), t) for kt, t in enumerate(ctx_half(f))]).then_inc(k1_mm, 1)

            def values0(k):
                if k == 0:
                    wait_lows(pe, f0_c, 0, F0_V, F0_V + 3)
                else:
                    pe.wait_ge(f0_added, NB if k >= 2 else NB - 1)
                    pe.wait_ge(v1_out, max(k - 1, 1))
                product(pe, bank[:, v0_bank(k), :], [(l, (w_v1[:, 0, kt, :], w_v1[:, 1, kt, :])) for kt, l in enumerate(ctx_tile(V_ORDER[k]))]
                        ).then_inc(v1_mm, 1)

            def zt(b):
                pe.wait_ge(z_gated, b + 1)
                if b >= 2:
                    pe.wait_ge(zt_low, b - 1)
                transposes(pe, 4 + b % 2, z[:, b, :]).then_inc(zt_mm, 1)

            wait_lows(pe, f0_c, 0, F0_K, F0_K)
            k0(1)
            zt(0)
            zt(1)
            pe.wait_ge(z_out, NB)
            values0(0)
            wait_lows(pe, f0_c, 0, F0_B, F0_B + 3)
            for b in range(NB):
                pe.wait_ge(zt_low, b + 1)
                if b >= 2:
                    pe.wait_ge(f0_added, b - 1)
                terms = [((z_t[:, b % 2, 0, kt * P:(kt + 1) * P], z_t[:, b % 2, 1, kt * P:(kt + 1) * P]),
                          (expert_out(kt, 0), expert_out(kt, 1))) for kt in range(KT)]
                product(pe, bank[:, 6 + b % 2, :], terms).then_inc(f0_mm, 1)
                if b + 2 < NB:
                    zt(b + 2)

            def qk(n, j, k, pieces=range(KT)):
                w = w_q1 if k < 2 else w_k1
                f = k % 2
                if pieces[0] == 0 and not (isinstance(n, int) and n == 0):
                    if k < 2:
                        pe.wait_ge(k1_out, 2 * n + f - 1)
                    else:
                        pe.wait_ge(q1_out, 2 * n + f + 1)
                tokens = xn_half(f) if k < 2 else ctx_half(f)
                mm = product(pe, bank[:, f, :], [(w_head(w, j % 2, kt), tokens[kt]) for kt in pieces],
                             first=pieces[0] == 0, final=pieces[-1] == KT - 1)
                if pieces[-1] == KT - 1:
                    mm.then_inc(q1_mm if k < 2 else k1_mm, 1)

            def values(g, b):
                pe.wait_ge(v1_out, 8 * g + b - 1)
                if b < 2:
                    pe.wait_ge(x1_added, 16 * g - 1 + b)
                product(pe, bank[:, 6 + b % 2, :], [(l, (w_v1[:, 0, kt, :], w_v1[:, 1, kt, :])) for kt, l in enumerate(ctx_tile(b))]
                        ).then_inc(v1_mm, 1)

            values0(1)
            values0(2)
            ln_transpose(pe, 2, 0, xw2, ln2_w)
            values0(3)
            ln_transpose(pe, 2, 1, xw2, ln2_w)
            wait_lows(pe, f0_c, 0, F0_X, F0_X + 3)
            k0(0)
            ln_transpose(pe, 2, 2, xw2, ln2_w)
            values0(4)
            ln_transpose(pe, 2, 3, xw2, ln2_w)
            values0(5)
            values0(6)
            ln_transpose(pe, 2, 4, xw2, ln2_w)
            ln_transpose(pe, 2, 5, xw2, ln2_w)
            wait_lows(pe, f0_c, 0, F0_Q, F0_Q)
            pe.wait_ge(ln_sems[2]["low"], 4)
            pe.wait_ge(k1_out, 2)
            qk(0, 0, 0)
            ln_transpose(pe, 2, 6, xw2, ln2_w)
            ln_transpose(pe, 2, 7, xw2, ln2_w)
            values0(7)
            pe.wait_ge(ln_sems[2]["low"], NB)
            qk(0, 0, 1)

            def group1(g, first, last):
                for j in range(GH):
                    n = 4 * g + j
                    head0 = first and j == 0
                    end = last and j == GH - 1
                    for f in range(2):
                        pe.wait_ge(q1_out, 2 * n + f + 1)
                        pe.wait_ge(k1_out, 2 * n + f + 1)
                        if not head0:
                            pe.wait_ge(s1_biased, 2 * n - 1 + f)
                        elif f == 0:
                            pe.wait_ge(ln_sems[2]["low"], NB)
                        for b in range(4):
                            at = (4 * f + b) * P
                            mm = pe.matmul(bank[:, 2 + f, b * P:(b + 1) * P], q_t1[:, j % 2, at:at + P], k_t1[:, j % 2, at:at + P],
                                           start=True, stop=True)
                        mm.then_inc(s1_mm, 1)
                    if not end:
                        def next_w(what):
                            k = "qk".index(what)
                            if first and j == 0:
                                wait_low(pe, f0_c, 0, F0_Q1 + k)
                            elif last and j >= 1:
                                wait_low(pe, l1e_c, 0, L1E[(j - 1, what)])
                            elif j == 0:
                                wait_low(pe, l1_c, g - 1, 13 + k)
                            else:
                                wait_low(pe, l1_c, g, 4 * j - 3 + k)

                        next_w("q")
                        qk(n + 1, j + 1, 0)
                        qk(n + 1, j + 1, 1)
                        next_w("k")
                        qk(n + 1, j + 1, 2, range(0, 2))
                    def half_out(b, h):
                        terms = [((o_t1[:, h, 0, b * P:(b + 1) * P], o_t1[:, h, 1, b * P:(b + 1) * P]), (w_o1[:, h, 0, :], w_o1[:, h, 1, :]))]
                        return product(pe, bank[:, LAST_BANKS[b], :], terms, first=h == 0, final=h == 1)

                    if end:
                        wait_low(pe, l1e_c, 0, L1E[(2, "o")])
                        pe.wait_ge(x1_added, 16 * g + 8)
                        for b in range(4):
                            half_out(b, 0)
                    for f in range(2):
                        pe.wait_ge(p1_norm, 2 * n + f + 1)
                        if not (head0 and f == 0):
                            pe.wait_ge(pt1_out, 2 * n + f)
                        transposes(pe, 4, p1[:, f].rearrange("p b n -> p (b n)")).then_inc(pt1_mm, 1)
                        if not end:
                            if f == 0:
                                qk(n + 1, j + 1, 2, range(2, 4))
                            else:
                                qk(n + 1, j + 1, 3)
                        if end:
                            pe.wait_ge(s1_biased, 2 * n + f + 1)
                            half_out(4 + f, 0)
                            if f == 1:
                                wait_low(pe, l1e_c, 0, L1E[(j, "o")])
                        pe.wait_ge(pt1_out, 2 * n + f + 1)
                        if not (head0 and f == 0):
                            pe.wait_ge(ot1_low, 2 * n + f)
                        if j == 0 and f == 0:
                            pe.wait_ge(v1_out, 8 * g + 8)
                        if end and f == 1:
                            for b in range(4):
                                pe.wait_ge(ot1_low, 2 * n + 1)
                                half_out(b, 1).then_inc(o1_mm, 1)
                        for b in range(4):
                            mm = pe.matmul(bank[:, 5, b * P:(b + 1) * P], v1[:, 4 * f + b, j * P:(j + 1) * P], p_t1[:, f, b * P:(b + 1) * P],
                                           start=True, stop=True)
                        mm.then_inc(pv1_mm, 1)
                    if j % 2 and not end:
                        if last:
                            wait_low(pe, l1e_c, 0, L1E[(j, "o")])
                        else:
                            wait_low(pe, l1_c, g, 4 * j)
                    for b in range(4 if end else 0, NB if j % 2 else 0):
                        pe.wait_ge(ot1_low, 2 * n + b // 4 + 1)
                        u = 16 * g + 8 * (j // 2) + b
                        if end and b < 6:
                            half_out(b, 1).then_inc(o1_mm, 1)
                            continue
                        if end:
                            pe.wait_ge(x1_added, u - 5)
                        elif not (first and j == 1 and b < 2):
                            pe.wait_ge(x1_added, u - 1)
                        if j == 1 and b < 2:
                            pe.wait_ge(v1_out, 8 * g + 8)
                        terms = [((o_t1[:, h, 0, b * P:(b + 1) * P], o_t1[:, h, 1, b * P:(b + 1) * P]), (w_o1[:, h, 0, :], w_o1[:, h, 1, :]))
                                 for h in range(2)]
                        product(pe, bank[:, 6 + b % 2, :], terms).then_inc(o1_mm, 1)
                    if j == GH - 1 and not last:
                        wait_lows(pe, l1_c, g, 15, 15)
                        for b in range(NB):
                            values(g + 1, b)
            groups(pe, group1)

            for b in range(4):
                ln_transpose(pe, 3, b)

            def gate_up(t, par, f):
                first = isinstance(t, int) and t == 0
                if f == 0:
                    pe.wait_ge(f1_low, 3 * t + 2)
                if first:
                    pe.wait_ge(ln_sems[3]["low"], 4 * f + 4)
                for k, w in enumerate((w_g, w_u)):
                    if first and f == 0 and k == 1:
                        ln_transpose(pe, 3, 4)
                        ln_transpose(pe, 3, 5)
                    if not first:
                        pe.wait_ge(h_done, 2 * t + f - 1)
                    terms = [((w[:, par, 0, kt * P:(kt + 1) * P], w[:, par, 1, kt * P:(kt + 1) * P]), r) for kt, r in enumerate(xn_half(f))]
                    product(pe, bank[:, 2 * f + k, :], terms).then_inc(ab_mm, 1)

            def down(t, par, b, reused=True):
                if reused:
                    pe.wait_ge(f1_added, NB * t + b - 3)
                pe.wait_ge(h_low, 2 * t + b // 4 + 1)
                product(pe, bank[:, 4 + b % 4, :], [((h_t[:, par, 0, b * P:(b + 1) * P], h_t[:, par, 1, b * P:(b + 1) * P]),
                                                     (w_d[:, par, 0, :], w_d[:, par, 1, :]))]).then_inc(f1_mm, 1)

            def tile(t, par):
                first = isinstance(t, int) and t == 0
                end = t if isinstance(t, int) else 1
                for f in range(2):
                    if first and f == 1:
                        ln_transpose(pe, 3, 6)
                        ln_transpose(pe, 3, 7)
                    if end < HT:
                        gate_up(t, par, f)
                    if f == 0 and not first:
                        pe.wait_ge(f1_low, 3 * t)
                    for b in range(4 * f, 4 * f + 4) if not first else ():
                        down(t - 1, 1 - par, b, not (isinstance(t, int) and t == 1 and f == 0))
            tiles(pe, tile)


def kernel(**inputs):
    import numpy as np
    import concourse.bacc as bacc
    from concourse.bass_utils import run_bass_kernel_spmd

    a = {k: np.asarray(v) for k, v in inputs.items()}

    def columns(w):
        return w.reshape(-1, D, KT, P).transpose(0, 2, 3, 1)

    def heads(w):
        return w.reshape(-1, P, KT, P).transpose(0, 3, 2, 1).reshape(-1, P, D)

    def outs(w):
        return w.reshape(D, -1, P).transpose(1, 2, 0)

    def filled(w, rows):
        full = np.zeros((rows,) + w.shape[1:], w.dtype)
        full[: w.shape[0]] = w
        return full

    def both(w):
        return np.stack([w, w], axis=1).reshape(-1)

    hidden = HT * P
    gate_up = {}
    for n in ("1", "3"):
        gate_up["p" + n] = heads(filled(both(a["L1_ffn_w" + n]).reshape(HID, D), hidden))
        gate_up["s" + n] = heads(filled(np.repeat(a["L1_ffn_s" + n], 64).reshape(HID, D), hidden))
    down_p = filled(both(a["L1_ffn_w2"]).reshape(D, HID).T, hidden).reshape(HT, P, D)
    down_s = filled(np.repeat(a["L1_ffn_s2"], 64).reshape(D, HID).T, hidden).reshape(HT, P, D)
    lower = (np.arange(P)[:, None] + HID * np.arange(4)[None, :]) % P >= 64
    arrays = {
        "x_in": a["x"],
        "mask0": a["mask_1x1xSxS2_ff0"].reshape(P, P),
        "mask1": a["mask_BxSxS2_bk0"].transpose(1, 0, 2),
        "ctx_t": a["ctx_4096"].reshape(2, HALF, KT, P).transpose(0, 2, 3, 1),
        "l0_q": columns(a["L0_xattn_Wq"]), "l0_k": columns(a["L0_xattn_Wk"]), "l0_v": columns(a["L0_xattn_Wv"]),
        "l0_o": outs(a["L0_xattn_Wo"]),
        "q_norm": a["L0_xattn_q_norm_w"].reshape(P, 1), "k_norm": a["L0_xattn_k_norm_w"].reshape(P, 1),
        "f0_a": columns(a["L0_ffn_A_w"]), "f0_b": columns(a["L0_ffn_B_w"]),
        "f0_r": heads(filled(a["L0_ffn_Wq_w"], P))[0], "f0_keys": a["L0_ffn_keys"].T,
        "bias": a["L1_xattn_position_bias"], "ln_w": a["L1_xattn_ln_weight"].reshape(1, D),
        "l1_q": heads(a["L1_xattn_w_q"]), "l1_k": heads(a["L1_xattn_w_k"]), "l1_v": columns(a["L1_xattn_w_v"]),
        "l1_o": outs(a["L1_xattn_w_out"]),
        "f1_p1": gate_up["p1"], "f1_s1": gate_up["s1"], "f1_p3": gate_up["p3"], "f1_s3": gate_up["s3"],
        "f1_p2": down_p, "f1_s2": down_s,
        "shift_l": np.where(lower, 28, 0).astype(np.int32), "shift_r": np.where(lower, 28, 4).astype(np.int32),
    }
    nc = bacc.Bacc("TRN2", target_bir_lowering=False, num_devices=1)
    feed, args = {}, {}
    for name, v in arrays.items():
        feed[name + "_dram"] = np.ascontiguousarray(v)
        args[name] = nc.dram_tensor(name + "_dram", v.shape, mybir.dt.from_np(v.dtype), kind="ExternalInput").ap()
    args["out"] = nc.dram_tensor("out_dram", (NB, P, D), F32, kind="ExternalOutput").ap()
    two_layer_block(nc, **args)
    r = run_bass_kernel_spmd(nc, [feed], core_ids=[0])
    return r.results[0]["out_dram"]
```
